# Optimizing a Trainium2 kernel written in Bass

```python
import numpy as np
import jax
import jax.numpy as jnp

def _softmax(x, axis=-1):
    return jax.nn.softmax(x, axis=axis)

def _gelu(x):
    return jax.nn.gelu(x, approximate=True)

def _silu(x):
    return jax.nn.silu(x)

def _sigmoid(x):
    return jax.nn.sigmoid(x)

def _layernorm(x, axis=-1, eps=1e-05):
    m = jnp.mean(x, axis=axis, keepdims=True)
    v = jnp.var(x, axis=axis, keepdims=True)
    return (x - m) / jnp.sqrt(v + eps)

def _scatter_add(tgt, idx, src, axis=0):
    return tgt.at[idx].add(src)

def _segment_sum(src, seg, n):
    return jax.ops.segment_sum(src, seg, n)
kernel_name = 'mk_recurrent_d1_jaxref_r2_c3c93b'

def setup_inputs(seed: int=0):
    np.random.seed(seed)
    _w = jnp.asarray

    def _L0_attn_setup():
        import jax, jax.numpy as jnp
        import numpy as np
        B, S, D, O = (8, 1024, 512, 512)
        key = jax.random.key(seed)
        k_in, k_a, k_bc = jax.random.split(key, 3)
        inputs = jax.random.normal(k_in, (B, S, D), dtype=jnp.float32)
        A = jax.random.uniform(k_a, (D,), minval=-0.99, maxval=0.99, dtype=jnp.float32)
        BC = jax.random.normal(k_bc, (D, O), dtype=jnp.float32) / D
        return {'inputs': inputs, 'A': A, 'BC': BC}
    _L0_attn_in = _L0_attn_setup()

    def _L0_ffn_setup():
        import jax, jax.numpy as jnp
        import numpy as np
        B, S, H, E = (2, 4096, 512, 8)
        SCALE = 0.5
        key = jax.random.key(seed)
        k1, k2 = jax.random.split(key)
        x = jax.random.normal(k1, (B, S, H), dtype=jnp.float32)
        gate_w = jax.random.normal(k2, (E, H), dtype=jnp.float32) * 0.02
        coeff = SCALE * (1.0 + 0.05 * jnp.arange(E, dtype=jnp.float32))
        expert_w = coeff[:, None, None] * jnp.eye(H, dtype=jnp.float32)
        return {'x': x, 'gate_w': gate_w, 'expert_w': expert_w}
    _L0_ffn_in = _L0_ffn_setup()
    _d = {'L0_attn_inputs': _L0_attn_in['inputs'], 'L0_attn_A': _L0_attn_in['A'], 'L0_attn_BC': _L0_attn_in['BC'], 'L0_ffn_gate_w': _L0_ffn_in['gate_w'], 'L0_ffn_expert_w': _L0_ffn_in['expert_w']}
    _x0 = _d['L0_attn_inputs']
    _d['L0_attn_inputs'] = jax.random.normal(jax.random.fold_in(jax.random.key(seed), 1), (4, 2048, 512), dtype=_x0.dtype)
    del _x0
    return _d

def reference(L0_attn_inputs, L0_attn_A, L0_attn_BC, L0_ffn_gate_w, L0_ffn_expert_w):

    def _L0_attn_ref(inputs, A, BC):
        import jax, jax.numpy as jnp
        import numpy as np
        B, S, D, O = (8, 1024, 512, 512)
        x_tfirst = jnp.swapaxes(inputs, 0, 1)

        def step(h, x_t):
            h = h * A + x_t
            return (h, h)
        h0 = jnp.zeros((inputs.shape[0], A.shape[0]), dtype=inputs.dtype)
        _, hs = jax.lax.scan(step, h0, x_tfirst)
        out = jnp.einsum('sbd,do->bso', hs, BC)
        return out

    def _L0_ffn_ref(x, gate_w, expert_w):
        import jax, jax.numpy as jnp
        import numpy as np
        B, S, H, E = (2, 4096, 512, 8)
        SCALE = 0.5
        scores = jnp.einsum('bsh,eh->bse', x, gate_w)
        chosen = jnp.argmax(scores, axis=-1)
        onehot = jax.nn.one_hot(chosen, gate_w.shape[0], dtype=x.dtype)
        expert_out = jnp.einsum('bsh,efh->bsef', x, expert_w)
        return x + jnp.einsum('bsef,bse->bsf', expert_out, onehot)
    x = L0_attn_inputs
    xn = _layernorm(x, axis=-1)
    s = _L0_attn_ref(xn, L0_attn_A, L0_attn_BC)
    g = _silu(_L0_ffn_ref(xn, L0_ffn_gate_w, L0_ffn_expert_w))
    x = x + s * g
    return x

_drawn_inputs = setup_inputs


def setup_inputs(seed=0):
    import zlib

    import numpy as np

    out = dict(_drawn_inputs(seed))
    spreads = {}
    factors = {}
    for name, (base, spread) in spreads.items():
        noise = np.random.default_rng([zlib.crc32(name.encode()), seed]).standard_normal(out[name].shape)
        drawn = base * np.exp(spread * noise) if base else spread * noise
        out[name] = jnp.asarray(drawn.astype(out[name].dtype))
    for name, factor in factors.items():
        out[name] = (out[name] * factor).astype(out[name].dtype)
    return out
```

```python
from contextlib import ExitStack

import numpy as np

import concourse.bass as bass
from concourse import mybir

ALU = mybir.AluOpType
ACT = mybir.ActivationFunctionType
AX = mybir.AxisListType
F32 = mybir.dt.float32
F32R = mybir.dt.float32r
BF16 = mybir.dt.bfloat16
I32 = mybir.dt.int32

P = 128
EPS = 1e-5


def bass_recurrent_routed(nc, x_in, a_in, bc_in, gate_in, expert_in, out):
    BATCH, SEQ, D = x_in.shape
    E = gate_in.shape[0]
    O = bc_in.shape[1]
    TOKENS = BATCH * SEQ
    CH = D // P
    TPG = 2
    GT = TPG * P
    GROUPS = TOKENS // GT
    GPB = SEQ // GT
    BLOCKS = E * CH
    TILES = -(-(TOKENS // P + E - 1) // 4) * 4
    ROW = D + O + 2
    TROWS = E * TOKENS // P + P
    EMPTY = TOKENS
    assert D == O and BLOCKS == GROUPS and CH == 4 and GPB % 4 == 0 and GROUPS % 4 == 0

    rows = nc.dram_tensor("token_rows", (TOKENS, ROW), F32).ap()
    table = nc.dram_tensor("slot_table", (TROWS, P), I32).ap()
    table_flat = table.rearrange("r q -> (r q)").unsqueeze(1)

    x_flat = x_in.rearrange("b s d -> (b s) d")
    x_g = x_flat.rearrange("(g t p) d -> g p t d", p=P, t=TPG)
    rows_g = rows.rearrange("(g t p) d -> g p t d", p=P, t=TPG)
    out_flat = out.rearrange("b s d -> (b s) d")
    w_e = expert_in.rearrange("e (c p) h -> e p c h", p=P)

    with ExitStack() as ctx:
        def sb(name, shape, dt):
            return ctx.enter_context(nc.sbuf_tensor(name, shape, dt))

        def sem(name):
            return ctx.enter_context(nc.semaphore(name))

        w_hi = sb("w_hi", [P, BLOCKS, D], F32R)
        w_lo = sb("w_lo", [P, BLOCKS, D], F32R)
        bc_hi = sb("bc_hi", [P, CH, O], F32R)
        bc_lo = sb("bc_lo", [P, CH, O], F32R)
        gate_t = sb("gate_t", [P, CH, E], F32)
        a_col = sb("a_col", [P, CH], F32)
        stream = sb("stream", [P, 5136], F32)
        hs = sb("hs", [P, 2, CH, GT], F32)
        split = sb("split", [P, 2, 2, CH * GT], F32R)
        s_out = sb("s_out", [P, 2, TPG, O + 2], F32)
        w_stage = sb("w_stage", [P, CH, D], F32)
        x_sb = stream[:, 0:2 * TPG * D].rearrange("p (v t d) -> p v t d", v=2, t=TPG)
        xn = stream[:, 2 * TPG * D:4 * TPG * D].rearrange("p (v t d) -> p v t d", v=2, t=TPG)
        xnt = stream[:, 4 * TPG * D:5 * TPG * D].rearrange("p (c n) -> p c n", c=CH)
        hs_hi = [split[:, v, 0, :].rearrange("p (c n) -> p c n", c=CH) for v in range(2)]
        hs_lo = [split[:, v, 1, :].rearrange("p (c n) -> p c n", c=CH) for v in range(2)]
        gate_raw = stream[0:E, 4 * TPG * D:4 * TPG * D + D]
        bc_raw = s_out[:, :, :, :].rearrange("p v t d -> p (v t d)")[:, 0:CH * O].rearrange("p (c o) -> p c o", c=CH)
        empty_ids = hs[:, :, :, :].rearrange("p v c n -> p (v c n)").bitcast(I32)[:, 0:TROWS]
        w_diag = w_stage[:, :, :].rearrange("p c d -> p (c d)")
        row_sb = [stream[:, u * ROW:(u + 1) * ROW] for u in range(4)]
        xn2 = [stream[:, 4 * ROW + 4 + v * D:4 * ROW + 4 + (v + 1) * D] for v in range(2)]
        x2_hi = [split[:, v, 0, 0:D] for v in range(2)]
        x2_lo = [split[:, v, 1, 0:D] for v in range(2)]
        g_sb = [hs[:, v, :, :].rearrange("p c n -> p (c n)")[:, 0:O] for v in range(2)]
        o_flat = s_out[:, :, :, :].rearrange("p v t d -> p (v t d)")
        o_sb = [o_flat[:, u * O:(u + 1) * O] for u in range(4)]
        scratch = w_stage[:, :, :].rearrange("p c d -> p (c d)")
        blk_i = scratch[:, 0:P].bitcast(I32)
        blk_f = scratch[:, P:2 * P]
        past = scratch[0:1, 512:512 + TILES * E].rearrange("p (j e) -> p j e", e=E)
        ident = sb("ident", [P, P], F32)
        before = sb("before", [P, P], BF16)
        ones = sb("ones", [P, P], BF16)
        ones_f = sb("ones_f", [P, E], F32)
        prio = sb("prio", [P, TPG, E], F32)
        e_base = sb("e_base", [P, E], BF16)
        token_id = sb("token_id", [P, 4, TPG], I32)
        id_step = sb("id_step", [P, TPG], I32)
        stats = sb("stats", [P, 2, 6], F32)
        mv = sb("mv", [P, 4, TPG, 2], F32)
        std = sb("std", [P, TPG], F32)
        r0 = sb("r0", [P, TPG], F32)
        rr = sb("rr", [P, TPG], F32)
        eps_col = sb("eps_col", [P, 1], F32)
        top = sb("top", [P, TPG], F32)
        ranked = sb("ranked", [P, TPG, E], F32)
        first = sb("first", [P, TPG], F32)
        onehot = sb("onehot", [P, 2, TPG, E], BF16)
        placed = sb("placed", [P, TPG, E], F32)
        slot_id = sb("slot_id", [P, 4, TPG], I32)
        seen = sb("seen", [P, 2, TPG, E], BF16)
        tile_i = sb("tile_i", [P, 2, E], I32)
        tile_f = sb("tile_f", [P, E], F32)
        tile_cum = sb("tile_cum", [P, E], F32)
        done = sb("done", [P, E], F32)
        done_n = sb("done_n", [P, E], F32)
        j_col = sb("j_col", [P, 1], F32)
        j_row = sb("j_row", [P, TILES], F32)
        pick = sb("pick", [P, 4], F32)
        blk_row = sb("blk_row", [P, 1], I32)
        e_row_f = sb("e_row_f", [1, TILES], F32)
        e_row = sb("e_row", [1, TILES], I32)
        slot_tok = sb("slot_tok", [P, TILES], I32)
        tok_cur = sb("tok_cur", [P, 4, 1], I32)

        def bank(name, n=1):
            return ctx.enter_context(nc.psum_tensor(name, [P, n, 512], F32))

        ps_xt = bank("ps_xt", 2)
        ps_s = bank("ps_s", 4)
        ps_gate = bank("ps_gate")
        ps_w = bank("ps_w")
        xt_ps = ps_xt[:, :, :].rearrange("p a b -> p (a b)").rearrange("p (c n) -> p c n", c=CH)
        score_ps = ps_gate[:, 0, 0:TPG * E].rearrange("p (t e) -> p t e", t=TPG)
        rank_ps = ps_gate[:, 0, 32:32 + TPG * E].rearrange("p (t e) -> p t e", t=TPG)
        gate_ps = ps_gate[:, 0, 64:64 + CH * E].rearrange("p (c e) -> p c e", c=CH)
        count_ps = ps_gate[:, 0, 96:96 + E]
        slot_ps = ps_gate[:, 0, 128:128 + P]
        w_ps = ps_w[:, 0, :]
        x2_ps = [ps_xt[:, v, :] for v in range(2)]
        z_ps = [ps_s[:, v, :] for v in range(2)]

        x_loaded = [sem(f"x_loaded{v}") for v in range(2)]
        x_stored = [sem(f"x_stored{v}") for v in range(2)]
        s_stored = [sem(f"s_stored{v}") for v in range(2)]
        a_loaded = sem("a_loaded")
        bc_loaded = sem("bc_loaded")
        gate_loaded = sem("gate_loaded")
        w_loaded = sem("w_loaded")
        table_empty = sem("table_empty")
        id_stored = [sem(f"id_stored{u}") for u in range(4)]
        blk_loaded = sem("blk_loaded")
        row_loaded = [sem(f"row_loaded{u}") for u in range(4)]
        out_stored = [sem(f"out_stored{u}") for u in range(4)]
        const_ready = sem("const_ready")
        empty_ready = sem("empty_ready")
        bc_hi_done = sem("bc_hi_done")
        bc_lo_done = sem("bc_lo_done")
        gate_turned = sem("gate_turned")
        gate_ready = sem("gate_ready")
        ln_step = sem("ln_step")
        var_ready = sem("var_ready")
        std_ready = sem("std_ready")
        rstd_ready = sem("rstd_ready")
        xn_ready = sem("xn_ready")
        xt_done = sem("xt_done")
        xnt_tail = sem("xnt_tail")
        xnt_ready = sem("xnt_ready")
        scan_done = sem("scan_done")
        hs_free = sem("hs_free")
        hi_done = sem("hi_done")
        lo_done = sem("lo_done")
        split_free = sem("split_free")
        s_done = sem("s_done")
        s_ps_free = sem("s_ps_free")
        stats_free = sem("stats_free")
        s_ready = sem("s_ready")
        score_done = sem("score_done")
        gate_step = sem("gate_step")
        onehot_ready = sem("onehot_ready")
        seen_ready = sem("seen_ready")
        rank_done = sem("rank_done")
        slot_ready = sem("slot_ready")
        id_ready = sem("id_ready")
        w_ready = sem("w_ready")
        wt_done = sem("wt_done")
        w_hi_done = sem("w_hi_done")
        w_lo_done = sem("w_lo_done")
        count_done = sem("count_done")
        plan_step = sem("plan_step")
        blk_row_ready = sem("blk_row_ready")
        e_row_ready = sem("e_row_ready")
        blk_f_ready = sem("blk_f_ready")
        slot_turned = sem("slot_turned")
        slot_tok_ready = sem("slot_tok_ready")
        tok_ready = sem("tok_ready")
        row_free = sem("row_free")
        xn2_ready = sem("xn2_ready")
        x2_done = sem("x2_done")
        x2_hi_done = sem("x2_hi_done")
        x2_lo_done = sem("x2_lo_done")
        z_done = sem("z_done")
        silu_done = sem("silu_done")
        prod_done = sem("prod_done")
        o_ready = sem("o_ready")

        block = ctx.enter_context(nc.Block())

        def rounds(U, it, c, ring):
            return (U // ring) * it + c // ring

        def wait(engine, semaphore, count):
            if not (isinstance(count, int) and count <= 0):
                engine.wait_ge(semaphore, count)

        @block.sync
        def _(sp):
            def load_x(it, c):
                nc.sync.dma_start(x_sb[:, c % 2], x_g[4 * it + c]).then_inc(x_loaded[c % 2], 16)

            def store_x(it, c):
                sp.wait_ge(x_loaded[c % 2], 16 * (rounds(4, it, c, 2) + 1))
                nc.sync.dma_start(rows_g[4 * it + c][:, :, 0:D], x_sb[:, c % 2]).then_inc(x_stored[c % 2], 16)

            def next_x(it, c):
                sp.wait_ge(xn_ready, 4 * it + c + 1)
                sp.wait_ge(x_stored[c % 2], 16 * (rounds(4, it, c, 2) + 1))
                load_x(it, c + 2)

            def store_s(it, c):
                sp.wait_ge(s_ready, 4 * it + c + 1)
                nc.sync.dma_start(rows_g[4 * it + c][:, :, D:ROW], s_out[:, c % 2]).then_inc(s_stored[c % 2], 16)

            def load_w(e):
                wait(sp, wt_done, CH * e)
                nc.sync.dma_start(w_stage[:, :, :], w_e[e]).then_inc(w_loaded, 16)

            load_x(0, 0)
            nc.sync.dma_start(gate_raw, gate_in).then_inc(gate_loaded, 16)
            with nc.allow_non_contiguous_dma(reason="512 decay factors, once"):
                nc.sync.dma_start(a_col[:, :], a_in.rearrange("(c p) -> p c", p=P)).then_inc(a_loaded, 16)
            nc.sync.dma_start(bc_raw, bc_in.rearrange("(c p) o -> p c o", p=P)).then_inc(bc_loaded, 16)
            load_x(0, 1)
            load_w(0)
            sp.wait_ge(empty_ready, 1)
            nc.sync.dma_start(table.rearrange("(p r) q -> p (r q)", p=P), empty_ids).then_inc(table_empty, 16)
            store_x(0, 0)
            next_x(0, 0)
            with sp.Fori(0, GROUPS // 4 - 1) as it:
                for c in range(1, 5):
                    store_x(it, c)
                    next_x(it, c)
                    if c == 3:
                        load_w(it + 1)
                    store_s(it, c - 1)
            for c in range(GROUPS - 3, GROUPS):
                store_x(0, c)
                if c + 2 < GROUPS:
                    next_x(0, c)
                store_s(0, c - 1)
            store_s(0, GROUPS - 1)

        @block.gpsimd
        def _(pool):
            pool.sem_inc(hs_free, 2)
            nc.gpsimd.memset(empty_ids, EMPTY).then_inc(empty_ready, 1)
            nc.gpsimd.memset(ident[:, :], 0.0).then_inc(const_ready, 1)
            nc.gpsimd.memset(before[:, :], 1.0).then_inc(const_ready, 1)
            nc.gpsimd.memset(ones[:, :], 1.0).then_inc(const_ready, 1)
            nc.gpsimd.memset(ones_f[:, :], 1.0).then_inc(const_ready, 1)
            nc.gpsimd.memset(id_step[:, :], 4 * GT).then_inc(const_ready, 1)
            nc.gpsimd.memset(eps_col[:, :], EPS).then_inc(const_ready, 1)
            nc.gpsimd.memset(seen[:, 0], 0.0).then_inc(const_ready, 1)
            nc.gpsimd.iota(prio[:, :, :], [[0, TPG], [-1, E]], base=E, channel_multiplier=0,
                           allow_small_or_imprecise_dtypes=True).then_inc(const_ready, 1)
            nc.gpsimd.iota(e_base[:, :], [[TOKENS // P, E]], base=0, channel_multiplier=0,
                           allow_small_or_imprecise_dtypes=True).then_inc(const_ready, 1)
            nc.gpsimd.iota(j_col[:, :], [[0, 1]], base=0, channel_multiplier=1,
                           allow_small_or_imprecise_dtypes=True).then_inc(const_ready, 1)
            nc.gpsimd.iota(j_row[:, :], [[1, TILES]], base=0, channel_multiplier=0,
                           allow_small_or_imprecise_dtypes=True).then_inc(const_ready, 1)
            nc.gpsimd.iota(token_id[:, :, :], [[GT, 4], [P, TPG]], base=-4 * GT,
                           channel_multiplier=1).then_inc(const_ready, 1)
            pool.wait_ge(const_ready, 12)
            nc.gpsimd.affine_select(out=ident[:, :], in_=ident[:, :], compare_op=ALU.not_equal, fill=1.0,
                                    base=0, pattern=[[-1, P]], channel_multiplier=1).then_inc(const_ready, 1)
            nc.gpsimd.affine_select(out=before[:, :], in_=before[:, :], compare_op=ALU.is_gt, fill=0.0,
                                    base=0, pattern=[[1, P]], channel_multiplier=-1).then_inc(const_ready, 1)
            pool.wait_ge(const_ready, 14)

            def add_identity(e):
                pool.wait_ge(w_loaded, 16 * (e + 1))
                for c in range(CH):
                    d = w_diag[:, c * (D + P):c * (D + P) + P]
                    last = nc.gpsimd.tensor_tensor(d, d, ident[:, :], ALU.add)
                last.then_inc(w_ready, 1)

            def count(it, c):
                pool.wait_ge(onehot_ready, 4 * it + c + 1)
                wait(pool, rank_done, 4 * it + c)
                wait(pool, seen_ready, 4 * it + c)
                nc.gpsimd.tensor_tensor(seen[:, (c + 1) % 2], seen[:, c % 2], onehot[:, c % 2],
                                        ALU.add).then_inc(seen_ready, 1)

            def low_part(it, c):
                pool.wait_ge(hi_done, 4 * it + c + 1)
                pool.wait_ge(split_free, 4 * it + c + 1)
                nc.gpsimd.tensor_tensor(hs_lo[c % 2], hs[:, c % 2], hs_hi[c % 2],
                                        ALU.subtract).then_inc(lo_done, 1)
                pool.wait_ge(lo_done, 4 * it + c + 1)
                pool.sem_inc(hs_free, 1)

            def scatter_ids(it, c):
                u = c % 4
                wait(pool, id_stored[u], 32 * rounds(4, it, c, 4))
                nc.gpsimd.tensor_tensor(token_id[:, u], token_id[:, u], id_step[:, :], ALU.add).then_inc(id_ready, 1)
                pool.wait_ge(table_empty, 16)
                pool.wait_ge(id_ready, 4 * it + c + 1)
                pool.wait_ge(slot_ready, 4 * it + c + 1)
                for t in range(TPG):
                    nc.gpsimd.indirect_dma_start(
                        out=table_flat, out_offset=bass.IndirectOffsetOnAxis(ap=slot_id[:, u, t:t + 1], axis=0),
                        in_=token_id[:, u, t:t + 1], in_offset=None,
                        bounds_check=E * TOKENS - 1, oob_is_err=False).then_inc(id_stored[u], 16)

            add_identity(0)

            def group(it, c):
                count(it, c)
                low_part(it, c)
                scatter_ids(it, c)

            for c in range(4):
                group(0, c)
            add_identity(1)
            with pool.Fori(1, GROUPS // 4 - 1) as it:
                for c in range(4):
                    group(it, c)
                add_identity(it + 1)
            for c in range(GROUPS - 4, GROUPS):
                group(0, c)

            for u in range(4):
                pool.wait_ge(id_stored[u], 32 * (GROUPS // 4))
            pool.wait_ge(blk_row_ready, 1)
            nc.gpsimd.indirect_dma_start(
                out=blk_i, out_offset=None, in_=table,
                in_offset=bass.IndirectOffsetOnAxis(ap=blk_row[:, 0:1], axis=0),
                bounds_check=TROWS - 1, oob_is_err=False).then_inc(blk_loaded, 16)

            def gather(it, c):
                u = c % 4
                n = 4 * it + c
                if not isinstance(it, int):
                    pool.to_reg(n + 1)
                pool.wait_ge(s_stored[1], 16 * (GROUPS // 2))
                pool.wait_ge(tok_ready, n + 1)
                pool.wait_ge(row_free, n + 1)
                nc.gpsimd.indirect_dma_start(
                    out=row_sb[u], out_offset=None, in_=rows,
                    in_offset=bass.IndirectOffsetOnAxis(ap=tok_cur[:, u], axis=0),
                    bounds_check=TOKENS - 1, oob_is_err=False).then_inc(row_loaded[u], 16)

            def scatter(it, c):
                u = c % 4
                n = 4 * it + c
                if not isinstance(it, int):
                    pool.to_reg(n + 1)
                pool.wait_ge(slot_tok_ready, 1)
                pool.wait_ge(o_ready, n + 1)
                nc.gpsimd.indirect_dma_start(
                    out=out_flat, out_offset=bass.IndirectOffsetOnAxis(ap=tok_cur[:, u], axis=0),
                    in_=o_sb[u], in_offset=None,
                    bounds_check=TOKENS - 1, oob_is_err=False).then_inc(out_stored[u], 16)

            for v in range(2):
                pool.wait_ge(x_stored[v], 16 * (GROUPS // 2))
                pool.wait_ge(s_stored[v], 16 * (GROUPS // 2))
            LEAD = 3
            for c in range(LEAD):
                gather(0, c)
            with pool.Fori(0, TILES // 4 - 1) as it:
                for c in range(4):
                    gather(it, c + LEAD)
                    scatter(it, c)
            for c in range(TILES - 4, TILES):
                if c + LEAD < TILES:
                    gather(0, c + LEAD)
                scatter(0, c)
            for u in range(4):
                pool.wait_ge(out_stored[u], 16 * (TILES // 4))

        @block.scalar
        def _(act):
            act.sem_inc(s_ps_free, 2)
            act.sem_inc(stats_free, 4)
            act.wait_ge(bc_loaded, 16)
            nc.scalar.copy(bc_hi[:, :, :], bc_raw).then_inc(bc_hi_done, 1)

            def root(it, c):
                act.wait_ge(var_ready, 4 * it + c + 1)
                wait(act, rstd_ready, 4 * it + c)
                nc.scalar.activation(std[:, :], mv[:, c % 4, :, 1], ACT.Sqrt, bias=eps_col[:, 0:1]).then_inc(std_ready, 1)

            def copy_xnt(it, c):
                act.wait_ge(xt_done, 4 * it + c + 1)
                wait(act, score_done, 4 * it + c)
                nc.scalar.copy(xnt[:, CH // 2:], xt_ps[:, CH // 2:]).then_inc(xnt_tail, 1)
                act.wait_ge(scan_done, CH * (4 * it + c) + CH // 2)
                nc.scalar.copy(xnt[:, :CH // 2], xt_ps[:, :CH // 2]).then_inc(xnt_ready, 1)

            def high_part(it, c):
                act.wait_ge(scan_done, CH * (4 * it + c + 1))
                act.wait_ge(split_free, 4 * it + c + 1)
                nc.scalar.copy(hs_hi[c % 2], hs[:, c % 2]).then_inc(hi_done, 1)

            def block_high(it, c):
                act.wait_ge(wt_done, 4 * it + c + 1)
                nc.scalar.copy(w_hi[:, 4 * it + c], w_ps).then_inc(w_hi_done, 1)

            def take_s(it, c):
                v = c % 2
                act.wait_ge(s_done, 4 * it + c + 1)
                wait(act, s_stored[v], 16 * rounds(4, it, c, 2))
                nc.scalar.copy(s_out[:, v, :, 0:O], ps_s[:, 2 * v:2 * v + 2, :]).then_inc(s_ps_free, 1)
                nc.scalar.copy(s_out[:, v, :, O:O + 2], mv[:, c % 4]).then_inc(stats_free, 1)
                act.wait_ge(s_ps_free, 4 * it + c + 3)
                act.wait_ge(stats_free, 4 * it + c + 5)
                act.sem_inc(s_ready, 1)

            act.wait_ge(const_ready, 14)
            root(0, 0)
            root(0, 1)
            copy_xnt(0, 0)
            high_part(0, 0)
            block_high(0, 0)
            root(0, 2)
            copy_xnt(0, 1)
            high_part(0, 1)
            block_high(0, 1)

            def group(it, c, more=True):
                if more:
                    root(it, c + 1)
                copy_xnt(it, c)
                take_s(it, c - 2)
                high_part(it, c)
                block_high(it, c)

            for c in range(2, 6):
                group(0, c)
            with act.Fori(1, GROUPS // 4 - 1) as it:
                for c in range(2, 6):
                    group(it, c)
            for c in range(GROUPS - 2, GROUPS):
                group(0, c, more=c + 1 < GROUPS)
            for c in range(GROUPS - 2, GROUPS):
                take_s(0, c)

            def high_x2(it, c):
                act.wait_ge(x2_done, 4 * it + c + 1)
                wait(act, z_done, 4 * it + c - 1)
                nc.scalar.copy(x2_hi[c % 2], x2_ps[c % 2]).then_inc(x2_hi_done, 1)

            def silu(it, c):
                act.wait_ge(z_done, 4 * it + c + 1)
                wait(act, prod_done, 4 * it + c - 1)
                nc.scalar.activation(g_sb[c % 2], z_ps[c % 2], ACT.Silu).then_inc(silu_done, 1)

            def tokens(it, c):
                u = c % 4
                wait(act, out_stored[u], 16 * rounds(4, it, c, 4))
                nc.scalar.copy(tok_cur[:, u], slot_tok[:, bass.ds(4 * it + c, 1)]).then_inc(tok_ready, 1)

            act.wait_ge(slot_tok_ready, 1)
            for c in range(4):
                tokens(0, c)
            high_x2(0, 0)
            high_x2(0, 1)
            silu(0, 0)
            high_x2(0, 2)
            silu(0, 1)
            with act.Fori(0, TILES // 4 - 1) as it:
                for c in range(3, 7):
                    high_x2(it, c)
                    tokens(it, c + 1)
                    silu(it, c - 1)
            high_x2(0, TILES - 1)
            silu(0, TILES - 2)
            silu(0, TILES - 1)

        @block.vector
        def _(dve):
            U = GPB
            dve.wait_ge(bc_hi_done, 1)
            nc.vector.tensor_tensor(bc_lo[:, :, :], bc_raw, bc_hi[:, :, :], ALU.subtract).then_inc(bc_lo_done, 1)

            def statistics(it, c):
                n = U * it + c
                v = c % 2
                dve.wait_ge(x_loaded[v], 16 * (rounds(U, it, c, 2) + 1))
                dve.wait_ge(stats_free, n + 1)
                for t in range(TPG):
                    last = nc.vector.bn_stats(stats[:, t, :], x_sb[:, v, t])
                last.then_inc(ln_step, 1)

            def variance(it, c):
                for t in range(TPG):
                    last = nc.vector.bn_aggr(mv[:, c % 4, t], stats[:, t, :])
                last.then_inc(var_ready, 1)

            def layernorm(it, c):
                n = U * it + c
                v = c % 2
                m = mv[:, c % 4]
                dve.wait_ge(std_ready, n + 1)
                nc.vector.reciprocal(r0[:, :], std[:, :]).then_inc(ln_step, 1)
                dve.wait_ge(ln_step, 5 * n + 2)
                nc.vector.tensor_tensor(rr[:, :], r0[:, :], r0[:, :], ALU.mult).then_inc(ln_step, 1)
                dve.wait_ge(ln_step, 5 * n + 3)
                nc.vector.scalar_tensor_tensor(rr[:, :], m[:, :, 1], EPS, rr[:, :], ALU.add,
                                               ALU.mult).then_inc(ln_step, 1)
                dve.wait_ge(ln_step, 5 * n + 4)
                nc.vector.tensor_scalar(rr[:, :], rr[:, :], -0.5, 1.5, ALU.mult, ALU.add).then_inc(ln_step, 1)
                dve.wait_ge(ln_step, 5 * n + 5)
                nc.vector.tensor_tensor(m[:, :, 1], r0[:, :], rr[:, :], ALU.mult).then_inc(rstd_ready, 1)
                dve.wait_ge(rstd_ready, n + 1)
                wait(dve, xt_done, n - 1)
                for t in range(TPG):
                    last = nc.vector.tensor_scalar(xn[:, v, t], x_sb[:, v, t], m[:, t, 0:1], m[:, t, 1:2],
                                                   ALU.subtract, ALU.mult)
                last.then_inc(xn_ready, 1)

            def scan(it, c, more):
                n = U * it + c
                v = c % 2
                dve.wait_ge(xt_done, n + 1)
                dve.wait_ge(hs_free, n + 1)
                wait(dve, scan_done, CH * n)
                if more:
                    dve.wait_ge(ln_step, 5 * (n + 1) + 1)
                for k in range(CH):
                    if k == CH // 2:
                        dve.wait_ge(xnt_tail, n + 1)
                    start = 0.0 if c % GPB == 0 else hs[:, 1 - v, k, GT - 1:GT]
                    nc.vector.tensor_tensor_scan(hs[:, v, k, :], a_col[:, k:k + 1].to_broadcast([P, GT]),
                                                 xt_ps[:, k, :], start, ALU.mult, ALU.add).then_inc(scan_done, 1)
                    if k == 0 and more:
                        variance(it, c + 1)

            def route(it, c):
                n = U * it + c
                v = c % 2
                dve.wait_ge(score_done, n + 1)
                nc.vector.tensor_reduce(top[:, :], score_ps, AX.X, ALU.max).then_inc(gate_step, 1)
                dve.wait_ge(gate_step, 4 * n + 1)
                for t in range(TPG):
                    last = nc.vector.scalar_tensor_tensor(ranked[:, t], score_ps[:, t], top[:, t:t + 1],
                                                          prio[:, t], ALU.is_equal, ALU.mult)
                last.then_inc(gate_step, 1)
                dve.wait_ge(gate_step, 4 * n + 2)
                nc.vector.tensor_reduce(first[:, :], ranked[:, :, :], AX.X, ALU.max).then_inc(gate_step, 1)
                dve.wait_ge(gate_step, 4 * n + 3)
                wait(dve, rank_done, n - 1)
                wait(dve, seen_ready, n - 1)
                for t in range(TPG):
                    last = nc.vector.tensor_scalar(onehot[:, v, t], ranked[:, t], first[:, t:t + 1], None,
                                                   ALU.is_equal)
                last.then_inc(onehot_ready, 1)

            def place(it, c):
                n = U * it + c
                u = c % 4
                dve.wait_ge(rank_done, n + 1)
                nc.vector.tensor_tensor(placed[:, :, :], rank_ps, onehot[:, c % 2], ALU.mult).then_inc(gate_step, 1)
                dve.wait_ge(gate_step, 4 * n + 4)
                wait(dve, id_stored[u], 32 * rounds(U, it, c, 4))
                with nc.allow_low_precision(reason="one whole number below 2**24 and zeros: the sum is exact"):
                    nc.vector.tensor_reduce(slot_id[:, u], placed[:, :, :], AX.X, ALU.add).then_inc(slot_ready, 1)

            def block_low(it, c):
                n = U * it + c
                dve.wait_ge(w_hi_done, n + 1)
                nc.vector.tensor_tensor(w_lo[:, n], w_ps, w_hi[:, n], ALU.subtract).then_inc(w_lo_done, 1)

            statistics(0, 0)
            dve.wait_ge(ln_step, 1)
            variance(0, 0)
            layernorm(0, 0)
            dve.wait_ge(gate_turned, 1)
            nc.vector.tensor_copy(gate_t[:, :, :], gate_ps).then_inc(gate_ready, 1)
            dve.wait_ge(const_ready, 14)
            dve.wait_ge(a_loaded, 16)
            dve.wait_ge(table_empty, 16)

            def group(it, c, more=True):
                if more:
                    statistics(it, c + 1)
                scan(it, c, more)
                if more:
                    layernorm(it, c + 1)
                route(it, c)
                block_low(it, c)
                place(it, c)

            for c in range(GPB):
                group(0, c)
            with dve.Fori(1, BATCH - 1) as b:
                for c in range(GPB):
                    group(b, c)
            for c in range(GROUPS - GPB, GROUPS):
                group(0, c, more=c + 1 < GROUPS)

            def step(ins, k):
                ins.then_inc(plan_step, 1)
                dve.wait_ge(plan_step, k)

            dve.wait_ge(count_done, 1)
            step(nc.vector.tensor_scalar(tile_i[:, 0], count_ps, float(P - 1), None, ALU.add), 1)
            step(nc.vector.tensor_scalar(tile_i[:, 1], tile_i[:, 0], P.bit_length() - 1, None,
                                         ALU.logical_shift_right), 2)
            step(nc.vector.tensor_copy(tile_f[:, :], tile_i[:, 1]), 3)
            step(nc.vector.tensor_tensor_scan(tile_cum[:, :], ones_f[:, :], tile_f[:, :], 0.0, ALU.mult, ALU.add), 4)
            step(nc.vector.tensor_scalar(done[:, :], tile_cum[:, :], j_col[:, 0:1], None, ALU.is_le), 5)
            nc.vector.tensor_reduce(pick[:, 0:1], done[:, :], AX.X, ALU.add)
            step(nc.vector.tensor_tensor(done_n[:, :], done[:, :], tile_f[:, :], ALU.mult), 6)
            step(nc.vector.tensor_reduce(pick[:, 1:2], done_n[:, :], AX.X, ALU.add), 7)
            step(nc.vector.tensor_scalar(pick[:, 2:3], pick[:, 0:1], float(TOKENS // P), j_col[:, 0:1],
                                         ALU.mult, ALU.add), 8)
            nc.vector.tensor_tensor(blk_row[:, :], pick[:, 2:3], pick[:, 1:2], ALU.subtract).then_inc(blk_row_ready, 1)
            step(nc.vector.tensor_tensor(
                past, tile_cum[0:1, :].unsqueeze(1).to_broadcast([1, TILES, E]),
                j_row[0:1, :].unsqueeze(2).to_broadcast([1, TILES, E]), ALU.is_le), 9)
            step(nc.vector.tensor_reduce(e_row_f[:, :], past, AX.X, ALU.add), 10)
            nc.vector.tensor_scalar(e_row[:, :], e_row_f[:, :], float(E - 1), None, ALU.min).then_inc(e_row_ready, 1)
            dve.wait_ge(blk_loaded, 16)
            nc.vector.tensor_copy(blk_f, blk_i).then_inc(blk_f_ready, 1)
            dve.wait_ge(slot_turned, 1)
            nc.vector.tensor_copy(slot_tok[:, :], slot_ps[:, 0:TILES]).then_inc(slot_tok_ready, 1)
            dve.sem_inc(row_free, 4)

            def normalise(it, c):
                u, v = c % 4, c % 2
                st = row_sb[u][:, D + O:ROW]
                dve.wait_ge(row_loaded[u], 16 * (rounds(4, it, c, 4) + 1))
                wait(dve, x2_done, 4 * it + c - 1)
                nc.vector.tensor_scalar(xn2[v], row_sb[u][:, 0:D], st[:, 0:1], st[:, 1:2],
                                        ALU.subtract, ALU.mult).then_inc(xn2_ready, 1)

            def low_x2(it, c):
                v = c % 2
                dve.wait_ge(x2_hi_done, 4 * it + c + 1)
                nc.vector.tensor_tensor(x2_lo[v], x2_ps[v], x2_hi[v], ALU.subtract).then_inc(x2_lo_done, 1)

            def combine(it, c):
                u, v = c % 4, c % 2
                dve.wait_ge(silu_done, 4 * it + c + 1)
                wait(dve, out_stored[u], 16 * rounds(4, it, c, 4))
                nc.vector.tensor_tensor(o_sb[u], row_sb[u][:, D:D + O], g_sb[v], ALU.mult).then_inc(prod_done, 1)
                dve.wait_ge(prod_done, 4 * it + c + 1)
                nc.vector.tensor_tensor(o_sb[u], o_sb[u], row_sb[u][:, 0:D], ALU.add).then_inc(o_ready, 1)
                dve.wait_ge(o_ready, 4 * it + c + 1)
                dve.sem_inc(row_free, 1)

            normalise(0, 0)
            normalise(0, 1)
            low_x2(0, 0)
            normalise(0, 2)
            low_x2(0, 1)
            combine(0, 0)

            def tile(it, c):
                normalise(it, c)
                low_x2(it, c - 1)
                combine(it, c - 2)

            for c in range(3, 7):
                tile(0, c)
            with dve.Fori(1, TILES // 4 - 1) as it:
                for c in range(3, 7):
                    tile(it, c)
            tile(0, TILES - 1)
            low_x2(0, TILES - 1)
            combine(0, TILES - 2)
            combine(0, TILES - 1)

        @block.tensor
        def _(pe):
            pe.sem_inc(split_free, 2)
            pe.wait_ge(const_ready, 14)

            def turn_x(it, c):
                pe.wait_ge(xn_ready, 4 * it + c + 1)
                wait(pe, scan_done, CH * (4 * it + c))
                wait(pe, xnt_ready, 4 * it + c)
                for t in range(TPG):
                    for k in range(CH):
                        last = nc.tensor.transpose(xt_ps[:, k, t * P:(t + 1) * P],
                                                   xn[:, c % 2, t, k * P:(k + 1) * P], ident[:, :])
                last.then_inc(xt_done, 1)

            def scores(it, c):
                pe.wait_ge(xnt_ready, 4 * it + c + 1)
                wait(pe, slot_ready, 4 * it + c)
                for t in range(TPG):
                    for k in range(CH):
                        last = nc.tensor.matmul(score_ps[:, t], xnt[:, k, t * P:(t + 1) * P], gate_t[:, k],
                                                start=(k == 0), stop=(k == CH - 1))
                last.then_inc(score_done, 1)

            def ranks(it, c):
                pe.wait_ge(onehot_ready, 4 * it + c + 1)
                wait(pe, seen_ready, 4 * it + c)
                wait(pe, slot_ready, 4 * it + c)
                for t in range(TPG):
                    terms = [(ones, e_base[:, :])] + [(ones, seen[:, c % 2, i]) for i in range(TPG)] \
                        + [(ones, onehot[:, c % 2, i]) for i in range(t)] + [(before, onehot[:, c % 2, t])]
                    for i, (left, right) in enumerate(terms):
                        last = nc.tensor.matmul(rank_ps[:, t], left[:, :], right, start=(i == 0),
                                                stop=(i == len(terms) - 1))
                last.then_inc(rank_done, 1)

            def turn_w(it, c):
                k = c % CH
                pe.wait_ge(w_ready, rounds(4, it, c, CH) + 1)
                wait(pe, w_lo_done, 4 * it + c)
                for f in range(CH):
                    last = nc.tensor.transpose(w_ps[:, f * P:(f + 1) * P], w_stage[:, f, k * P:(k + 1) * P],
                                               ident[:, :])
                last.then_inc(wt_done, 1)

            def product_hi(it, c):
                v = c % 2
                pe.wait_ge(hi_done, 4 * it + c + 1)
                pe.wait_ge(s_ps_free, 4 * it + c + 1)
                for t in range(TPG):
                    for k in range(CH):
                        left = hs_hi[v][:, k, t * P:(t + 1) * P]
                        nc.tensor.matmul(ps_s[:, 2 * v + t], left, bc_hi[:, k], start=(k == 0), stop=False)
                        nc.tensor.matmul(ps_s[:, 2 * v + t], left, bc_lo[:, k], start=False, stop=False)

            def product_lo(it, c):
                v = c % 2
                pe.wait_ge(lo_done, 4 * it + c + 1)
                for t in range(TPG):
                    for k in range(CH):
                        last = nc.tensor.matmul(ps_s[:, 2 * v + t], hs_lo[v][:, k, t * P:(t + 1) * P], bc_hi[:, k],
                                                start=False, stop=(k == CH - 1))
                last.then_inc(s_done, 1)
                pe.wait_ge(s_done, 4 * it + c + 1)
                pe.sem_inc(split_free, 1)

            pe.wait_ge(gate_loaded, 16)
            for k in range(CH):
                last = nc.tensor.transpose(gate_ps[:, k], gate_raw[:, k * P:(k + 1) * P], ident[0:E, 0:E])
            last.then_inc(gate_turned, 1)
            turn_x(0, 0)
            pe.wait_ge(gate_ready, 1)
            scores(0, 0)
            turn_w(0, 0)
            ranks(0, 0)
            pe.wait_ge(bc_lo_done, 1)

            def group(it, c):
                turn_x(it, c + 1)
                product_hi(it, c)
                scores(it, c + 1)
                product_lo(it, c)
                turn_w(it, c + 1)
                ranks(it, c + 1)

            with pe.Fori(0, GROUPS // 4 - 1) as it:
                for c in range(4):
                    group(it, c)
            for c in range(GROUPS - 4, GROUPS - 1):
                group(0, c)
            pe.wait_ge(seen_ready, GROUPS)
            pe.wait_ge(slot_ready, GROUPS)
            for i in range(TPG):
                last = nc.tensor.matmul(count_ps, ones[:, :], seen[:, GROUPS % 2, i], start=(i == 0),
                                        stop=(i == TPG - 1))
            last.then_inc(count_done, 1)
            product_hi(0, GROUPS - 1)
            product_lo(0, GROUPS - 1)
            pe.wait_ge(blk_f_ready, 1)
            nc.tensor.transpose(slot_ps, blk_f, ident[:, :]).then_inc(slot_turned, 1)

            def turn_x2(it, c):
                v = c % 2
                pe.wait_ge(xn2_ready, 4 * it + c + 1)
                wait(pe, x2_lo_done, 4 * it + c - 1)
                for k in range(CH):
                    last = nc.tensor.transpose(x2_ps[v][:, k * P:(k + 1) * P], xn2[v][:, k * P:(k + 1) * P],
                                               ident[:, :])
                last.then_inc(x2_done, 1)

            def expert(it, c):
                v = c % 2
                e = nc.tensor.value_load(e_row[0:1, bass.ds(4 * it + c, 1)], min_val=0, max_val=E - 1)
                pe.wait_ge(x2_lo_done, 4 * it + c + 1)
                wait(pe, silu_done, 4 * it + c - 1)
                for k in range(CH):
                    hi, lo = x2_hi[v][:, k * P:(k + 1) * P], x2_lo[v][:, k * P:(k + 1) * P]
                    wh, wl = w_hi[:, e * CH + k], w_lo[:, e * CH + k]
                    nc.tensor.matmul(z_ps[v], hi, wh, start=(k == 0), stop=False)
                    nc.tensor.matmul(z_ps[v], hi, wl, start=False, stop=False)
                    last = nc.tensor.matmul(z_ps[v], lo, wh, start=False, stop=(k == CH - 1))
                last.then_inc(z_done, 1)

            pe.wait_ge(e_row_ready, 1)
            pe.wait_ge(w_lo_done, BLOCKS)
            turn_x2(0, 0)
            turn_x2(0, 1)
            expert(0, 0)
            turn_x2(0, 2)
            expert(0, 1)
            with pe.Fori(0, TILES // 4 - 1) as it:
                for c in range(3, 7):
                    turn_x2(it, c)
                    expert(it, c - 1)
            turn_x2(0, TILES - 1)
            expert(0, TILES - 2)
            expert(0, TILES - 1)


_INS = ["L0_attn_inputs", "L0_attn_A", "L0_attn_BC", "L0_ffn_gate_w", "L0_ffn_expert_w"]


def kernel(**inputs):
    import numpy as _np
    import concourse.bacc as _bacc
    from concourse import mybir as _mybir
    from concourse.bass_utils import run_bass_kernel_spmd as _run

    nc = _bacc.Bacc("TRN2", target_bir_lowering=False, num_devices=1)
    arrays, args = {}, []
    for name in _INS:
        a = _np.ascontiguousarray(inputs[name])
        arrays[f"in_{name}_dram"] = a
        args.append(nc.dram_tensor(f"in_{name}_dram", a.shape, _mybir.dt.from_np(a.dtype), kind="ExternalInput").ap())
    shape = inputs["L0_attn_inputs"].shape
    out = nc.dram_tensor("out_0_dram", shape, _mybir.dt.float32, kind="ExternalOutput").ap()
    bass_recurrent_routed(nc, *args, out)
    r = _run(nc, [arrays], core_ids=[0])
    return r.results[0]["out_0_dram"]
```

```python
from contextlib import ExitStack

import numpy as np

import concourse.bass as bass
from concourse import mybir

ALU = mybir.AluOpType
ACT = mybir.ActivationFunctionType
AX = mybir.AxisListType
F32 = mybir.dt.float32
F32R = mybir.dt.float32r
BF16 = mybir.dt.bfloat16
I32 = mybir.dt.int32

P = 128
EPS = 1e-5


def bass_recurrent_routed(nc, x_in, a_in, bc_in, gate_in, expert_in, out):
    BATCH, SEQ, D = x_in.shape
    E = gate_in.shape[0]
    O = bc_in.shape[1]
    TOKENS = BATCH * SEQ
    CH = D // P
    TPG = 2
    GT = TPG * P
    GROUPS = TOKENS // GT
    GPB = SEQ // GT
    BLOCKS = E * CH
    TILES = TOKENS // P + E - 1
    XR = 4
    RR = 6
    OR = 3
    LOOPS = TILES // RR - 1
    ROW = D + O + 2
    TROWS = E * TOKENS // P + P
    EMPTY = TOKENS
    assert D == O and BLOCKS == GROUPS and CH == 4 and GPB % 4 == 0 and GROUPS % 4 == 0

    rows = nc.dram_tensor("token_rows", (TOKENS, ROW), F32).ap()
    table = nc.dram_tensor("slot_table", (TROWS, P), I32).ap()
    table_flat = table.rearrange("r q -> (r q)").unsqueeze(1)

    x_flat = x_in.rearrange("b s d -> (b s) d")
    x_g = x_flat.rearrange("(g t p) d -> g p t d", p=P, t=TPG)
    rows_g = rows.rearrange("(g t p) d -> g p t d", p=P, t=TPG)
    out_flat = out.rearrange("b s d -> (b s) d")
    w_e = expert_in.rearrange("e (c p) h -> e p c h", p=P)

    with ExitStack() as ctx:
        def sb(name, shape, dt):
            return ctx.enter_context(nc.sbuf_tensor(name, shape, dt))

        def sem(name):
            return ctx.enter_context(nc.semaphore(name))

        w_hi = sb("w_hi", [P, BLOCKS, D], F32R)
        w_lo = sb("w_lo", [P, BLOCKS, D], F32R)
        bc_hi = sb("bc_hi", [P, CH, O], F32R)
        bc_lo = sb("bc_lo", [P, CH, O], F32R)
        gate_t = sb("gate_t", [P, CH, E], F32)
        a_col = sb("a_col", [P, CH], F32)
        split = sb("split", [P, 2, 2, CH * GT], F32R)
        SIZES = {"x": XR * TPG * D, "xnt": CH * GT, "hs": 2 * CH * GT, "s": 2 * TPG * (O + 2), "w": CH * D}
        work = sb("work", [P, sum(SIZES.values())], F32)
        at = dict(zip(SIZES, np.cumsum([0, *SIZES.values()]).tolist()))

        def part(start, *shape):
            flat = work[:, start:start + int(np.prod(shape))]
            names = "abcd"[:len(shape)]
            if len(shape) == 1:
                return flat
            return flat.rearrange(f"p ({' '.join(names)}) -> p {' '.join(names)}", **dict(zip(names, shape)))

        x_sb = part(at["x"], XR, TPG, D)
        xnt = part(at["xnt"], CH, GT)
        hs = part(at["hs"], 2, CH, GT)
        s_out = part(at["s"], 2, TPG, O + 2)
        w_stage = part(at["w"], CH, D)
        w_flat = part(at["w"], CH * D)
        hs_hi = [split[:, v, 0, :].rearrange("p (c n) -> p c n", c=CH) for v in range(2)]
        hs_lo = [split[:, v, 1, :].rearrange("p (c n) -> p c n", c=CH) for v in range(2)]
        gate_raw = work[0:E, at["xnt"]:at["xnt"] + D]
        bc_raw = part(at["s"], CH, O)
        empty_ids = part(at["hs"], TROWS).bitcast(I32)
        row_sb = part(0, RR, ROW)
        xn2 = part(RR * ROW, 2, D)
        g_sb = part(RR * ROW + 2 * D, 2, O)
        o_sb = part(RR * ROW + 2 * D + 2 * O, OR, O)
        plan_at = RR * ROW + 2 * D + (2 + OR) * O
        blk_f = part(plan_at, P)
        blk_i = part(plan_at + P, P).bitcast(I32)
        past = part(plan_at + 2 * P, TILES, E)[0:1]
        assert plan_at >= at["w"] and plan_at + 2 * P + TILES * E <= sum(SIZES.values())
        x2_hi = [split[:, v, 0, 0:D] for v in range(2)]
        x2_lo = [split[:, v, 1, 0:D] for v in range(2)]
        ident = sb("ident", [P, P], F32)
        before = sb("before", [P, P], BF16)
        ones = sb("ones", [P, P], BF16)
        ones_f = sb("ones_f", [P, E], F32)
        prio = sb("prio", [P, TPG, E], F32)
        e_base = sb("e_base", [P, E], BF16)
        token_id = sb("token_id", [P, 4, TPG], I32)
        id_step = sb("id_step", [P, TPG], I32)
        stats = sb("stats", [P, 2, 6], F32)
        mv = sb("mv", [P, 4, TPG, 2], F32)
        std2 = sb("std2", [P, TPG], F32)
        half = sb("half", [P, TPG], F32)
        std = sb("std", [P, TPG], F32)
        shift = sb("shift", [P, 2, TPG], F32)
        eps_col = sb("eps_col", [P, 1], F32)
        top = sb("top", [P, TPG], F32)
        ranked = sb("ranked", [P, TPG, E], F32)
        first = sb("first", [P, TPG], F32)
        onehot = sb("onehot", [P, 2, TPG, E], BF16)
        placed = sb("placed", [P, TPG, E], F32)
        slot_id = sb("slot_id", [P, 4, TPG], I32)
        seen = sb("seen", [P, 2, TPG, E], BF16)
        tile_i = sb("tile_i", [P, 2, E], I32)
        tile_f = sb("tile_f", [P, E], F32)
        tile_cum = sb("tile_cum", [P, E], F32)
        done = sb("done", [P, E], F32)
        done_n = sb("done_n", [P, E], F32)
        j_col = sb("j_col", [P, 1], F32)
        j_row = sb("j_row", [P, TILES], F32)
        pick = sb("pick", [P, 4], F32)
        blk_row = sb("blk_row", [P, 1], I32)
        e_row_f = sb("e_row_f", [1, TILES], F32)
        e_row = sb("e_row", [1, TILES], I32)
        slot_tok = sb("slot_tok", [P, TILES], I32)
        tok_in = sb("tok_in", [P, RR, 1], I32)
        tok_out = sb("tok_out", [P, OR, 1], I32)

        def bank(name, n=1):
            return ctx.enter_context(nc.psum_tensor(name, [P, n, 512], F32))

        ps_xt = bank("ps_xt", 2)
        ps_s = bank("ps_s", 4)
        ps_gate = bank("ps_gate")
        ps_w = bank("ps_w")
        xt_ps = ps_xt[:, :, :].rearrange("p a b -> p (a b)").rearrange("p (c n) -> p c n", c=CH)
        score_ps = ps_gate[:, 0, 0:TPG * E].rearrange("p (t e) -> p t e", t=TPG)
        rank_ps = ps_gate[:, 0, 32:32 + TPG * E].rearrange("p (t e) -> p t e", t=TPG)
        gate_ps = ps_gate[:, 0, 64:64 + CH * E].rearrange("p (c e) -> p c e", c=CH)
        count_ps = ps_gate[:, 0, 96:96 + E]
        slot_ps = ps_gate[:, 0, 128:128 + P]
        w_ps = ps_w[:, 0, :]
        x2_ps = [ps_xt[:, v, :] for v in range(2)]
        z_ps = [ps_s[:, v, :] for v in range(2)]

        x_loaded = [sem(f"x_loaded{v}") for v in range(XR)]
        x_copied = sem("x_copied")
        s_stored = [sem(f"s_stored{v}") for v in range(2)]
        a_loaded = sem("a_loaded")
        bc_loaded = sem("bc_loaded")
        gate_loaded = sem("gate_loaded")
        w_loaded = sem("w_loaded")
        table_empty = sem("table_empty")
        id_stored = [sem(f"id_stored{u}") for u in range(4)]
        blk_loaded = sem("blk_loaded")
        row_loaded = [sem(f"row_loaded{u}") for u in range(RR)]
        out_stored = [sem(f"out_stored{u}") for u in range(OR)]
        const_ready = sem("const_ready")
        empty_ready = sem("empty_ready")
        bc_hi_done = sem("bc_hi_done")
        bc_lo_done = sem("bc_lo_done")
        gate_turned = sem("gate_turned")
        gate_ready = sem("gate_ready")
        ln_step = sem("ln_step")
        var_ready = sem("var_ready")
        std_ready = sem("std_ready")
        shift_ready = sem("shift_ready")
        xn_ready = sem("xn_ready")
        xt_done = sem("xt_done")
        xnt_tail = sem("xnt_tail")
        xnt_ready = sem("xnt_ready")
        scan_done = sem("scan_done")
        hs_free = sem("hs_free")
        hi_done = sem("hi_done")
        lo_done = sem("lo_done")
        split_free = sem("split_free")
        s_done = sem("s_done")
        s_ps_free = sem("s_ps_free")
        stats_free = sem("stats_free")
        s_ready = sem("s_ready")
        score_done = sem("score_done")
        gate_step = sem("gate_step")
        onehot_ready = sem("onehot_ready")
        seen_ready = sem("seen_ready")
        rank_done = sem("rank_done")
        slot_ready = sem("slot_ready")
        id_ready = sem("id_ready")
        w_ready = sem("w_ready")
        wt_done = sem("wt_done")
        w_hi_done = sem("w_hi_done")
        w_lo_done = sem("w_lo_done")
        count_done = sem("count_done")
        plan_step = sem("plan_step")
        blk_row_ready = sem("blk_row_ready")
        e_row_ready = sem("e_row_ready")
        blk_f_ready = sem("blk_f_ready")
        slot_turned = sem("slot_turned")
        slot_tok_ready = sem("slot_tok_ready")
        tok_in_ready = sem("tok_in_ready")
        tok_out_ready = sem("tok_out_ready")
        row_free = sem("row_free")
        xn2_ready = sem("xn2_ready")
        x2_done = sem("x2_done")
        x2_hi_done = sem("x2_hi_done")
        x2_lo_done = sem("x2_lo_done")
        z_done = sem("z_done")
        silu_done = sem("silu_done")
        prod_done = sem("prod_done")
        o_ready = sem("o_ready")

        block = ctx.enter_context(nc.Block())

        def rounds(U, it, c, ring):
            return (U // ring) * it + c // ring

        def wait(engine, semaphore, count):
            if not (isinstance(count, int) and count <= 0):
                engine.wait_ge(semaphore, count)

        @block.sync
        def _(sp):
            def load_x(it, c):
                nc.sync.dma_start(x_sb[:, c % XR], x_g[4 * it + c]).then_inc(x_loaded[c % XR], 16)

            def next_x(it, c):
                sp.wait_ge(xt_done, 4 * it + c + 1)
                load_x(it, c + XR)

            def copy_x(it, c):
                nc.sync.dma_start(rows_g[4 * it + c][:, :, 0:D], x_g[4 * it + c]).then_inc(x_copied, 16)

            def store_s(it, c):
                sp.wait_ge(s_ready, 4 * it + c + 1)
                nc.sync.dma_start(rows_g[4 * it + c][:, :, D:ROW], s_out[:, c % 2]).then_inc(s_stored[c % 2], 16)

            def load_w(e):
                wait(sp, wt_done, CH * e)
                nc.sync.dma_start(w_stage, w_e[e]).then_inc(w_loaded, 16)

            load_x(0, 0)
            nc.sync.dma_start(gate_raw, gate_in).then_inc(gate_loaded, 16)
            with nc.allow_non_contiguous_dma(reason="512 decay factors, once"):
                nc.sync.dma_start(a_col[:, :], a_in.rearrange("(c p) -> p c", p=P)).then_inc(a_loaded, 16)
            nc.sync.dma_start(bc_raw, bc_in.rearrange("(c p) o -> p c o", p=P)).then_inc(bc_loaded, 16)
            load_x(0, 1)
            load_w(0)
            sp.wait_ge(empty_ready, 1)
            nc.sync.dma_start(table.rearrange("(p r) q -> p (r q)", p=P), empty_ids).then_inc(table_empty, 16)
            load_x(0, 2)
            load_x(0, 3)
            with sp.Fori(0, GROUPS // 4 - 1) as it:
                for c in range(4):
                    next_x(it, c)
                    copy_x(it, c)
                    if c == 2:
                        load_w(it + 1)
                    store_s(it, c)
            for c in range(GROUPS - 4, GROUPS):
                copy_x(0, c)
                store_s(0, c)

        @block.gpsimd
        def _(pool):
            pool.sem_inc(hs_free, 2)
            nc.gpsimd.memset(empty_ids, EMPTY).then_inc(empty_ready, 1)
            nc.gpsimd.memset(ident[:, :], 0.0).then_inc(const_ready, 1)
            nc.gpsimd.memset(before[:, :], 1.0).then_inc(const_ready, 1)
            nc.gpsimd.memset(ones[:, :], 1.0).then_inc(const_ready, 1)
            nc.gpsimd.memset(ones_f[:, :], 1.0).then_inc(const_ready, 1)
            nc.gpsimd.memset(id_step[:, :], 4 * GT).then_inc(const_ready, 1)
            nc.gpsimd.memset(eps_col[:, :], 4 * EPS).then_inc(const_ready, 1)
            nc.gpsimd.memset(seen[:, 0], 0.0).then_inc(const_ready, 1)
            nc.gpsimd.iota(prio[:, :, :], [[0, TPG], [-1, E]], base=E, channel_multiplier=0,
                           allow_small_or_imprecise_dtypes=True).then_inc(const_ready, 1)
            nc.gpsimd.iota(e_base[:, :], [[TOKENS // P, E]], base=0, channel_multiplier=0,
                           allow_small_or_imprecise_dtypes=True).then_inc(const_ready, 1)
            nc.gpsimd.iota(j_col[:, :], [[0, 1]], base=0, channel_multiplier=1,
                           allow_small_or_imprecise_dtypes=True).then_inc(const_ready, 1)
            nc.gpsimd.iota(j_row[:, :], [[1, TILES]], base=0, channel_multiplier=0,
                           allow_small_or_imprecise_dtypes=True).then_inc(const_ready, 1)
            nc.gpsimd.iota(token_id[:, :, :], [[GT, 4], [P, TPG]], base=-4 * GT,
                           channel_multiplier=1).then_inc(const_ready, 1)
            pool.wait_ge(const_ready, 12)
            nc.gpsimd.affine_select(out=ident[:, :], in_=ident[:, :], compare_op=ALU.not_equal, fill=1.0,
                                    base=0, pattern=[[-1, P]], channel_multiplier=1).then_inc(const_ready, 1)
            nc.gpsimd.affine_select(out=before[:, :], in_=before[:, :], compare_op=ALU.is_gt, fill=0.0,
                                    base=0, pattern=[[1, P]], channel_multiplier=-1).then_inc(const_ready, 1)
            pool.wait_ge(const_ready, 14)

            def add_identity(e):
                pool.wait_ge(w_loaded, 16 * (e + 1))
                for c in range(CH):
                    d = w_flat[:, c * (D + P):c * (D + P) + P]
                    last = nc.gpsimd.tensor_tensor(d, d, ident[:, :], ALU.add)
                last.then_inc(w_ready, 1)

            def count(it, c):
                pool.wait_ge(onehot_ready, 4 * it + c + 1)
                wait(pool, rank_done, 4 * it + c)
                wait(pool, seen_ready, 4 * it + c)
                nc.gpsimd.tensor_tensor(seen[:, (c + 1) % 2], seen[:, c % 2], onehot[:, c % 2],
                                        ALU.add).then_inc(seen_ready, 1)

            def low_part(it, c):
                pool.wait_ge(hi_done, 4 * it + c + 1)
                pool.wait_ge(split_free, 4 * it + c + 1)
                nc.gpsimd.tensor_tensor(hs_lo[c % 2], hs[:, c % 2], hs_hi[c % 2],
                                        ALU.subtract).then_inc(lo_done, 1)
                pool.wait_ge(lo_done, 4 * it + c + 1)
                pool.sem_inc(hs_free, 1)

            def scatter_ids(it, c):
                u = c % 4
                wait(pool, id_stored[u], 32 * rounds(4, it, c, 4))
                nc.gpsimd.tensor_tensor(token_id[:, u], token_id[:, u], id_step[:, :], ALU.add).then_inc(id_ready, 1)
                pool.wait_ge(table_empty, 16)
                pool.wait_ge(id_ready, 4 * it + c + 1)
                pool.wait_ge(slot_ready, 4 * it + c + 1)
                for t in range(TPG):
                    nc.gpsimd.indirect_dma_start(
                        out=table_flat, out_offset=bass.IndirectOffsetOnAxis(ap=slot_id[:, u, t:t + 1], axis=0),
                        in_=token_id[:, u, t:t + 1], in_offset=None,
                        bounds_check=E * TOKENS - 1, oob_is_err=False).then_inc(id_stored[u], 16)

            add_identity(0)

            def group(it, c):
                count(it, c)
                low_part(it, c)
                scatter_ids(it, c)

            for c in range(4):
                group(0, c)
            add_identity(1)
            with pool.Fori(1, GROUPS // 4 - 1) as it:
                for c in range(4):
                    group(it, c)
                add_identity(it + 1)
            for c in range(GROUPS - 4, GROUPS):
                group(0, c)

            for u in range(4):
                pool.wait_ge(id_stored[u], 32 * (GROUPS // 4))
            pool.wait_ge(blk_row_ready, 1)
            nc.gpsimd.indirect_dma_start(
                out=blk_i, out_offset=None, in_=table,
                in_offset=bass.IndirectOffsetOnAxis(ap=blk_row[:, 0:1], axis=0),
                bounds_check=TROWS - 1, oob_is_err=False).then_inc(blk_loaded, 16)

            def gather(it, c):
                u = c % RR
                n = RR * it + c
                if not isinstance(it, int):
                    pool.to_reg(n + 1)
                pool.wait_ge(x_copied, 16 * GROUPS)
                pool.wait_ge(tok_in_ready, n + 1)
                pool.wait_ge(row_free, n + 1)
                nc.gpsimd.indirect_dma_start(
                    out=row_sb[:, u], out_offset=None, in_=rows,
                    in_offset=bass.IndirectOffsetOnAxis(ap=tok_in[:, u], axis=0),
                    bounds_check=TOKENS - 1, oob_is_err=False).then_inc(row_loaded[u], 16)

            def scatter(it, c):
                u = c % OR
                n = RR * it + c
                if not isinstance(it, int):
                    pool.to_reg(n + 1)
                pool.wait_ge(slot_tok_ready, 1)
                pool.wait_ge(tok_out_ready, n + 1)
                pool.wait_ge(o_ready, n + 1)
                nc.gpsimd.indirect_dma_start(
                    out=out_flat, out_offset=bass.IndirectOffsetOnAxis(ap=tok_out[:, u], axis=0),
                    in_=o_sb[:, u], in_offset=None,
                    bounds_check=TOKENS - 1, oob_is_err=False).then_inc(out_stored[u], 16)

            for v in range(2):
                pool.wait_ge(s_stored[v], 16 * (GROUPS // 2))
            for c in range(RR):
                gather(0, c)
            with pool.Fori(0, LOOPS) as it:
                for c in range(RR):
                    scatter(it, c)
                    gather(it, c + RR)
            for c in range(RR * LOOPS, TILES):
                scatter(0, c)
                if c + RR < TILES:
                    gather(0, c + RR)
            for u in range(OR):
                pool.wait_ge(out_stored[u], 16 * len(range(u, TILES, OR)))

        @block.scalar
        def _(act):
            act.sem_inc(s_ps_free, 2)
            act.sem_inc(stats_free, 4)
            act.wait_ge(bc_loaded, 16)
            nc.scalar.copy(bc_hi[:, :, :], bc_raw).then_inc(bc_hi_done, 1)

            def root(it, c):
                act.wait_ge(var_ready, 4 * it + c + 1)
                wait(act, shift_ready, 4 * it + c)
                nc.scalar.activation(std2[:, :], mv[:, c % 4, :, 1], ACT.Sqrt, bias=eps_col[:, 0:1],
                                     scale=4.0).then_inc(std_ready, 1)

            def normalise(it, c):
                act.wait_ge(shift_ready, 4 * it + c + 1)
                for t in range(TPG):
                    xt = x_sb[:, c % XR, t]
                    last = nc.scalar.activation(xt, xt, ACT.Identity, bias=shift[:, c % 2, t:t + 1],
                                                scale=mv[:, c % 4, t, 1:2])
                last.then_inc(xn_ready, 1)

            def copy_tail(it, c):
                act.wait_ge(xt_done, 4 * it + c + 1)
                wait(act, score_done, 4 * it + c)
                nc.scalar.copy(xnt[:, CH // 2:], xt_ps[:, CH // 2:]).then_inc(xnt_tail, 1)

            def copy_head(it, c):
                act.wait_ge(scan_done, CH * (4 * it + c) + CH // 2)
                nc.scalar.copy(xnt[:, :CH // 2], xt_ps[:, :CH // 2]).then_inc(xnt_ready, 1)

            def high_part(it, c):
                act.wait_ge(scan_done, CH * (4 * it + c + 1))
                act.wait_ge(split_free, 4 * it + c + 1)
                nc.scalar.copy(hs_hi[c % 2], hs[:, c % 2]).then_inc(hi_done, 1)

            def block_high(it, c):
                act.wait_ge(wt_done, 4 * it + c + 1)
                nc.scalar.copy(w_hi[:, 4 * it + c], w_ps).then_inc(w_hi_done, 1)

            def take_s(it, c):
                v = c % 2
                act.wait_ge(s_done, 4 * it + c + 1)
                wait(act, s_stored[v], 16 * rounds(4, it, c, 2))
                nc.scalar.copy(s_out[:, v, :, 0:O], ps_s[:, 2 * v:2 * v + 2, :]).then_inc(s_ps_free, 1)
                nc.scalar.copy(s_out[:, v, :, O:O + 2], mv[:, c % 4]).then_inc(stats_free, 1)
                act.wait_ge(s_ps_free, 4 * it + c + 3)
                act.wait_ge(stats_free, 4 * it + c + 5)
                act.sem_inc(s_ready, 1)

            act.wait_ge(const_ready, 14)
            root(0, 0)
            normalise(0, 0)

            def group(it, c, more=True, back=True):
                copy_tail(it, c)
                if more:
                    root(it, c + 1)
                copy_head(it, c)
                high_part(it, c)
                if more:
                    normalise(it, c + 1)
                if back:
                    take_s(it, c - 2)
                block_high(it, c)

            for c in range(6):
                group(0, c, back=c >= 2)
            with act.Fori(1, GROUPS // 4 - 1) as it:
                for c in range(2, 6):
                    group(it, c)
            for c in range(GROUPS - 2, GROUPS):
                group(0, c, more=c + 1 < GROUPS)
            for c in range(GROUPS - 2, GROUPS):
                take_s(0, c)

            def high_x2(it, c):
                act.wait_ge(x2_done, RR * it + c + 1)
                wait(act, z_done, RR * it + c - 1)
                nc.scalar.copy(x2_hi[c % 2], x2_ps[c % 2]).then_inc(x2_hi_done, 1)

            def silu(it, c):
                act.wait_ge(z_done, RR * it + c + 1)
                wait(act, prod_done, RR * it + c - 1)
                nc.scalar.activation(g_sb[:, c % 2], z_ps[c % 2], ACT.Silu).then_inc(silu_done, 1)

            def ids_in(it, c):
                wait(act, row_loaded[c % RR], 16 * rounds(RR, it, c, RR))
                nc.scalar.copy(tok_in[:, c % RR], slot_tok[:, bass.ds(RR * it + c, 1)]).then_inc(tok_in_ready, 1)

            def ids_out(it, c):
                wait(act, out_stored[c % OR], 16 * rounds(RR, it, c, OR))
                nc.scalar.copy(tok_out[:, c % OR], slot_tok[:, bass.ds(RR * it + c, 1)]).then_inc(tok_out_ready, 1)

            def tile(it, c, ahead=True):
                silu(it, c)
                high_x2(it, c + 2)
                ids_out(it, c)
                if ahead:
                    ids_in(it, c + RR)

            act.wait_ge(slot_tok_ready, 1)
            for c in range(RR):
                ids_in(0, c)
            high_x2(0, 0)
            high_x2(0, 1)
            for c in range(RR):
                tile(0, c)
            with act.Fori(1, LOOPS) as it:
                for c in range(RR):
                    tile(it, c)
            for c in range(RR * LOOPS, TILES - 2):
                tile(0, c, ahead=c + RR < TILES)
            for c in range(TILES - 2, TILES):
                silu(0, c)
                ids_out(0, c)

        @block.vector
        def _(dve):
            U = GPB
            dve.wait_ge(bc_hi_done, 1)
            nc.vector.tensor_tensor(bc_lo[:, :, :], bc_raw, bc_hi[:, :, :], ALU.subtract).then_inc(bc_lo_done, 1)

            def statistics(it, c):
                n = U * it + c
                dve.wait_ge(x_loaded[c % XR], 16 * (rounds(U, it, c, XR) + 1))
                dve.wait_ge(stats_free, n + 1)
                for t in range(TPG):
                    last = nc.vector.bn_stats(stats[:, t, :], x_sb[:, c % XR, t])
                last.then_inc(ln_step, 1)

            def variance(it, c):
                for t in range(TPG):
                    last = nc.vector.bn_aggr(mv[:, c % 4, t], stats[:, t, :])
                last.then_inc(var_ready, 1)

            def deviation(it, c):
                n = U * it + c
                m = mv[:, c % 4]
                dve.wait_ge(std_ready, n + 1)
                nc.vector.reciprocal(half[:, :], std2[:, :]).then_inc(ln_step, 1)
                dve.wait_ge(ln_step, 5 * n + 2)
                nc.vector.scalar_tensor_tensor(half[:, :], m[:, :, 1], EPS, half[:, :], ALU.add,
                                               ALU.mult).then_inc(ln_step, 1)
                dve.wait_ge(ln_step, 5 * n + 3)
                nc.vector.scalar_tensor_tensor(std[:, :], std2[:, :], 0.25, half[:, :], ALU.mult,
                                               ALU.add).then_inc(ln_step, 1)
                dve.wait_ge(ln_step, 5 * n + 4)
                nc.vector.reciprocal(m[:, :, 1], std[:, :]).then_inc(ln_step, 1)
                dve.wait_ge(ln_step, 5 * n + 5)
                wait(dve, xn_ready, n - 1)
                nc.vector.scalar_tensor_tensor(shift[:, c % 2], m[:, :, 0], -1.0, m[:, :, 1], ALU.mult,
                                               ALU.mult).then_inc(shift_ready, 1)

            def scan(it, c, more):
                n = U * it + c
                v = c % 2
                dve.wait_ge(xt_done, n + 1)
                dve.wait_ge(hs_free, n + 1)
                wait(dve, scan_done, CH * n)
                if more:
                    dve.wait_ge(ln_step, 5 * (n + 1) + 1)
                for k in range(CH):
                    if k == CH // 2:
                        dve.wait_ge(xnt_tail, n + 1)
                    start = 0.0 if c % GPB == 0 else hs[:, 1 - v, k, GT - 1:GT]
                    nc.vector.tensor_tensor_scan(hs[:, v, k, :], a_col[:, k:k + 1].to_broadcast([P, GT]),
                                                 xt_ps[:, k, :], start, ALU.mult, ALU.add).then_inc(scan_done, 1)
                    if k == 0 and more:
                        variance(it, c + 1)

            def route(it, c):
                n = U * it + c
                v = c % 2
                dve.wait_ge(score_done, n + 1)
                nc.vector.tensor_reduce(top[:, :], score_ps, AX.X, ALU.max).then_inc(gate_step, 1)
                dve.wait_ge(gate_step, 4 * n + 1)
                for t in range(TPG):
                    last = nc.vector.scalar_tensor_tensor(ranked[:, t], score_ps[:, t], top[:, t:t + 1],
                                                          prio[:, t], ALU.is_equal, ALU.mult)
                last.then_inc(gate_step, 1)
                dve.wait_ge(gate_step, 4 * n + 2)
                nc.vector.tensor_reduce(first[:, :], ranked[:, :, :], AX.X, ALU.max).then_inc(gate_step, 1)
                dve.wait_ge(gate_step, 4 * n + 3)
                wait(dve, rank_done, n - 1)
                wait(dve, seen_ready, n - 1)
                for t in range(TPG):
                    last = nc.vector.tensor_scalar(onehot[:, v, t], ranked[:, t], first[:, t:t + 1], None,
                                                   ALU.is_equal)
                last.then_inc(onehot_ready, 1)

            def place(it, c):
                n = U * it + c
                u = c % 4
                dve.wait_ge(rank_done, n + 1)
                nc.vector.tensor_tensor(placed[:, :, :], rank_ps, onehot[:, c % 2], ALU.mult).then_inc(gate_step, 1)
                dve.wait_ge(gate_step, 4 * n + 4)
                wait(dve, id_stored[u], 32 * rounds(U, it, c, 4))
                with nc.allow_low_precision(reason="one whole number below 2**24 and zeros: the sum is exact"):
                    nc.vector.tensor_reduce(slot_id[:, u], placed[:, :, :], AX.X, ALU.add).then_inc(slot_ready, 1)

            def block_low(it, c):
                n = U * it + c
                dve.wait_ge(w_hi_done, n + 1)
                nc.vector.tensor_tensor(w_lo[:, n], w_ps, w_hi[:, n], ALU.subtract).then_inc(w_lo_done, 1)

            statistics(0, 0)
            dve.wait_ge(ln_step, 1)
            variance(0, 0)
            deviation(0, 0)
            dve.wait_ge(gate_turned, 1)
            nc.vector.tensor_copy(gate_t[:, :, :], gate_ps).then_inc(gate_ready, 1)
            dve.wait_ge(const_ready, 14)
            dve.wait_ge(a_loaded, 16)
            dve.wait_ge(table_empty, 16)

            def group(it, c, more=True, back=True):
                if more:
                    statistics(it, c + 1)
                scan(it, c, more)
                if back:
                    place(it, c - 1)
                if more:
                    deviation(it, c + 1)
                route(it, c)
                block_low(it, c)

            for c in range(GPB):
                group(0, c, back=c >= 1)
            with dve.Fori(1, BATCH - 1) as b:
                for c in range(GPB):
                    group(b, c)
            for c in range(GROUPS - GPB, GROUPS):
                group(0, c, more=c + 1 < GROUPS)
            place(0, GROUPS - 1)

            def step(ins, k):
                ins.then_inc(plan_step, 1)
                dve.wait_ge(plan_step, k)

            dve.wait_ge(count_done, 1)
            step(nc.vector.tensor_scalar(tile_i[:, 0], count_ps, float(P - 1), None, ALU.add), 1)
            step(nc.vector.tensor_scalar(tile_i[:, 1], tile_i[:, 0], P.bit_length() - 1, None,
                                         ALU.logical_shift_right), 2)
            step(nc.vector.tensor_copy(tile_f[:, :], tile_i[:, 1]), 3)
            step(nc.vector.tensor_tensor_scan(tile_cum[:, :], ones_f[:, :], tile_f[:, :], 0.0, ALU.mult, ALU.add), 4)
            step(nc.vector.tensor_scalar(done[:, :], tile_cum[:, :], j_col[:, 0:1], None, ALU.is_le), 5)
            nc.vector.tensor_reduce(pick[:, 0:1], done[:, :], AX.X, ALU.add)
            step(nc.vector.tensor_tensor(done_n[:, :], done[:, :], tile_f[:, :], ALU.mult), 6)
            step(nc.vector.tensor_reduce(pick[:, 1:2], done_n[:, :], AX.X, ALU.add), 7)
            step(nc.vector.tensor_scalar(pick[:, 2:3], pick[:, 0:1], float(TOKENS // P), j_col[:, 0:1],
                                         ALU.mult, ALU.add), 8)
            nc.vector.tensor_tensor(blk_row[:, :], pick[:, 2:3], pick[:, 1:2], ALU.subtract).then_inc(blk_row_ready, 1)
            step(nc.vector.tensor_tensor(
                past, tile_cum[0:1, :].unsqueeze(1).to_broadcast([1, TILES, E]),
                j_row[0:1, :].unsqueeze(2).to_broadcast([1, TILES, E]), ALU.is_le), 9)
            step(nc.vector.tensor_reduce(e_row_f[:, :], past, AX.X, ALU.add), 10)
            nc.vector.tensor_scalar(e_row[:, :], e_row_f[:, :], float(E - 1), None, ALU.min).then_inc(e_row_ready, 1)
            dve.wait_ge(blk_loaded, 16)
            nc.vector.tensor_copy(blk_f, blk_i).then_inc(blk_f_ready, 1)
            dve.wait_ge(slot_turned, 1)
            nc.vector.tensor_copy(slot_tok[:, :], slot_ps[:, 0:TILES]).then_inc(slot_tok_ready, 1)
            dve.sem_inc(row_free, RR)

            def normalise(it, c):
                row = row_sb[:, c % RR]
                dve.wait_ge(row_loaded[c % RR], 16 * (rounds(RR, it, c, RR) + 1))
                wait(dve, x2_done, RR * it + c - 1)
                nc.vector.tensor_scalar(xn2[:, c % 2], row[:, 0:D], row[:, D + O:D + O + 1], row[:, D + O + 1:ROW],
                                        ALU.subtract, ALU.mult).then_inc(xn2_ready, 1)

            def low_x2(it, c):
                dve.wait_ge(x2_hi_done, RR * it + c + 1)
                nc.vector.tensor_tensor(x2_lo[c % 2], x2_ps[c % 2], x2_hi[c % 2],
                                        ALU.subtract).then_inc(x2_lo_done, 1)

            def product(it, c):
                dve.wait_ge(silu_done, RR * it + c + 1)
                wait(dve, out_stored[c % OR], 16 * rounds(RR, it, c, OR))
                nc.vector.tensor_tensor(o_sb[:, c % OR], row_sb[:, c % RR, D:D + O], g_sb[:, c % 2],
                                        ALU.mult).then_inc(prod_done, 1)

            def residual(it, c):
                dve.wait_ge(prod_done, RR * it + c + 1)
                nc.vector.tensor_tensor(o_sb[:, c % OR], o_sb[:, c % OR], row_sb[:, c % RR, 0:D],
                                        ALU.add).then_inc(o_ready, 1)

            def release(it, c):
                dve.wait_ge(o_ready, RR * it + c + 1)
                dve.sem_inc(row_free, 1)

            def tile(it, c, ahead=3, back=True):
                if ahead >= 2:
                    low_x2(it, c + 2)
                product(it, c)
                if ahead >= 3:
                    normalise(it, c + 3)
                residual(it, c)
                release(it, c)

            normalise(0, 0)
            normalise(0, 1)
            low_x2(0, 0)
            normalise(0, 2)
            low_x2(0, 1)
            for c in range(RR):
                tile(0, c)
            with dve.Fori(1, LOOPS) as it:
                for c in range(RR):
                    tile(it, c)
            for c in range(RR * LOOPS, TILES):
                tile(0, c, ahead=TILES - 1 - c)

        @block.tensor
        def _(pe):
            pe.sem_inc(split_free, 2)
            pe.wait_ge(const_ready, 14)

            def turn_x(it, c):
                pe.wait_ge(xn_ready, 4 * it + c + 1)
                wait(pe, scan_done, CH * (4 * it + c))
                wait(pe, xnt_ready, 4 * it + c)
                for t in range(TPG):
                    for k in range(CH):
                        last = nc.tensor.transpose(xt_ps[:, k, t * P:(t + 1) * P],
                                                   x_sb[:, c % XR, t, k * P:(k + 1) * P], ident[:, :])
                last.then_inc(xt_done, 1)

            def scores(it, c):
                pe.wait_ge(xnt_ready, 4 * it + c + 1)
                wait(pe, slot_ready, 4 * it + c)
                for t in range(TPG):
                    for k in range(CH):
                        last = nc.tensor.matmul(score_ps[:, t], xnt[:, k, t * P:(t + 1) * P], gate_t[:, k],
                                                start=(k == 0), stop=(k == CH - 1))
                last.then_inc(score_done, 1)

            def ranks(it, c):
                pe.wait_ge(onehot_ready, 4 * it + c + 1)
                wait(pe, seen_ready, 4 * it + c)
                wait(pe, slot_ready, 4 * it + c)
                for t in range(TPG):
                    terms = [(ones, e_base[:, :])] + [(ones, seen[:, c % 2, i]) for i in range(TPG)] \
                        + [(ones, onehot[:, c % 2, i]) for i in range(t)] + [(before, onehot[:, c % 2, t])]
                    for i, (left, right) in enumerate(terms):
                        last = nc.tensor.matmul(rank_ps[:, t], left[:, :], right, start=(i == 0),
                                                stop=(i == len(terms) - 1))
                last.then_inc(rank_done, 1)

            def turn_w(it, c):
                k = c % CH
                pe.wait_ge(w_ready, rounds(4, it, c, CH) + 1)
                wait(pe, w_lo_done, 4 * it + c)
                for f in range(CH):
                    last = nc.tensor.transpose(w_ps[:, f * P:(f + 1) * P], w_stage[:, f, k * P:(k + 1) * P],
                                               ident[:, :])
                last.then_inc(wt_done, 1)

            def product_hi(it, c):
                v = c % 2
                pe.wait_ge(hi_done, 4 * it + c + 1)
                pe.wait_ge(s_ps_free, 4 * it + c + 1)
                for t in range(TPG):
                    for k in range(CH):
                        left = hs_hi[v][:, k, t * P:(t + 1) * P]
                        nc.tensor.matmul(ps_s[:, 2 * v + t], left, bc_hi[:, k], start=(k == 0), stop=False)
                        nc.tensor.matmul(ps_s[:, 2 * v + t], left, bc_lo[:, k], start=False, stop=False)

            def product_lo(it, c):
                v = c % 2
                pe.wait_ge(lo_done, 4 * it + c + 1)
                for t in range(TPG):
                    for k in range(CH):
                        last = nc.tensor.matmul(ps_s[:, 2 * v + t], hs_lo[v][:, k, t * P:(t + 1) * P], bc_hi[:, k],
                                                start=False, stop=(k == CH - 1))
                last.then_inc(s_done, 1)
                pe.wait_ge(s_done, 4 * it + c + 1)
                pe.sem_inc(split_free, 1)

            pe.wait_ge(gate_loaded, 16)
            for k in range(CH):
                last = nc.tensor.transpose(gate_ps[:, k], gate_raw[:, k * P:(k + 1) * P], ident[0:E, 0:E])
            last.then_inc(gate_turned, 1)
            turn_x(0, 0)
            pe.wait_ge(gate_ready, 1)
            scores(0, 0)
            turn_w(0, 0)
            pe.wait_ge(bc_lo_done, 1)

            def group(it, c):
                turn_x(it, c + 1)
                ranks(it, c)
                product_hi(it, c)
                scores(it, c + 1)
                product_lo(it, c)
                turn_w(it, c + 1)

            for c in range(4):
                group(0, c)
            with pe.Fori(1, GROUPS // 4 - 1) as it:
                for c in range(4):
                    group(it, c)
            for c in range(GROUPS - 4, GROUPS - 1):
                group(0, c)
            ranks(0, GROUPS - 1)
            pe.wait_ge(seen_ready, GROUPS)
            pe.wait_ge(slot_ready, GROUPS)
            for i in range(TPG):
                last = nc.tensor.matmul(count_ps, ones[:, :], seen[:, GROUPS % 2, i], start=(i == 0),
                                        stop=(i == TPG - 1))
            last.then_inc(count_done, 1)
            product_hi(0, GROUPS - 1)
            product_lo(0, GROUPS - 1)
            pe.wait_ge(blk_f_ready, 1)
            nc.tensor.transpose(slot_ps, blk_f, ident[:, :]).then_inc(slot_turned, 1)

            def turn_x2(it, c):
                v = c % 2
                pe.wait_ge(xn2_ready, RR * it + c + 1)
                wait(pe, x2_lo_done, RR * it + c - 1)
                for k in range(CH):
                    last = nc.tensor.transpose(x2_ps[v][:, k * P:(k + 1) * P], xn2[:, v, k * P:(k + 1) * P],
                                               ident[:, :])
                last.then_inc(x2_done, 1)

            def expert(it, c):
                v = c % 2
                e = nc.tensor.value_load(e_row[0:1, bass.ds(RR * it + c, 1)], min_val=0, max_val=E - 1)
                pe.wait_ge(x2_lo_done, RR * it + c + 1)
                wait(pe, silu_done, RR * it + c - 1)
                for k in range(CH):
                    hi, lo = x2_hi[v][:, k * P:(k + 1) * P], x2_lo[v][:, k * P:(k + 1) * P]
                    wh, wl = w_hi[:, e * CH + k], w_lo[:, e * CH + k]
                    nc.tensor.matmul(z_ps[v], hi, wh, start=(k == 0), stop=False)
                    nc.tensor.matmul(z_ps[v], hi, wl, start=False, stop=False)
                    last = nc.tensor.matmul(z_ps[v], lo, wh, start=False, stop=(k == CH - 1))
                last.then_inc(z_done, 1)

            def tile(it, c, ahead=True):
                if ahead:
                    turn_x2(it, c + 1)
                expert(it, c)

            pe.wait_ge(e_row_ready, 1)
            pe.wait_ge(w_lo_done, BLOCKS)
            turn_x2(0, 0)
            for c in range(RR):
                tile(0, c)
            with pe.Fori(1, LOOPS) as it:
                for c in range(RR):
                    tile(it, c)
            for c in range(RR * LOOPS, TILES):
                tile(0, c, ahead=c + 1 < TILES)


_INS = ["L0_attn_inputs", "L0_attn_A", "L0_attn_BC", "L0_ffn_gate_w", "L0_ffn_expert_w"]


def kernel(**inputs):
    import numpy as _np
    import concourse.bacc as _bacc
    from concourse import mybir as _mybir
    from concourse.bass_utils import run_bass_kernel_spmd as _run

    nc = _bacc.Bacc("TRN2", target_bir_lowering=False, num_devices=1)
    arrays, args = {}, []
    for name in _INS:
        a = _np.ascontiguousarray(inputs[name])
        arrays[f"in_{name}_dram"] = a
        args.append(nc.dram_tensor(f"in_{name}_dram", a.shape, _mybir.dt.from_np(a.dtype), kind="ExternalInput").ap())
    shape = inputs["L0_attn_inputs"].shape
    out = nc.dram_tensor("out_0_dram", shape, _mybir.dt.float32, kind="ExternalOutput").ap()
    bass_recurrent_routed(nc, *args, out)
    r = _run(nc, [arrays], core_ids=[0])
    return r.results[0]["out_0_dram"]
```

```python
from contextlib import ExitStack

import numpy as np

import concourse.bass as bass
from concourse import mybir

ALU = mybir.AluOpType
ACT = mybir.ActivationFunctionType
AX = mybir.AxisListType
F32 = mybir.dt.float32
F32R = mybir.dt.float32r
BF16 = mybir.dt.bfloat16
I32 = mybir.dt.int32

P = 128
EPS = 1e-5


def bass_recurrent_routed(nc, x_in, a_in, bc_in, gate_in, expert_in, out):
    BATCH, SEQ, D = x_in.shape
    E = gate_in.shape[0]
    O = bc_in.shape[1]
    TOKENS = BATCH * SEQ
    CH = D // P
    TPG = 2
    GT = TPG * P
    GROUPS = TOKENS // GT
    GPB = SEQ // GT
    BLOCKS = E * CH
    TILES = TOKENS // P + E - 1
    XR = 4
    WR = 2
    RR = 6
    OR = 3
    LOOPS = TILES // RR - 1
    ROW = D + O + 2
    TROWS = E * TOKENS // P + P
    LATE = 2
    LAST = (GROUPS - 1) % 2
    EMPTY = TOKENS
    assert D == O and BLOCKS == GROUPS and CH == 4 and WR == 2 and GPB % 4 == 0 and GROUPS % 4 == 0

    rows = nc.dram_tensor("token_rows", (TOKENS, ROW), F32).ap()
    table = nc.dram_tensor("slot_table", (TROWS, P), I32).ap()
    table_flat = table.rearrange("r q -> (r q)").unsqueeze(1)

    x_flat = x_in.rearrange("b s d -> (b s) d")
    x_g = x_flat.rearrange("(g t p) d -> g p t d", p=P, t=TPG)
    rows_g = rows.rearrange("(g t p) d -> g p t d", p=P, t=TPG)
    out_flat = out.rearrange("b s d -> (b s) d")
    w_e = expert_in.rearrange("e (f p) (c q) -> e c p f q", p=P, q=P)

    with ExitStack() as ctx:
        def sb(name, shape, dt):
            return ctx.enter_context(nc.sbuf_tensor(name, shape, dt))

        def sem(name):
            return ctx.enter_context(nc.semaphore(name))

        w_hi = sb("w_hi", [P, BLOCKS, D], F32R)
        w_lo = sb("w_lo", [P, BLOCKS, D], F32R)
        bc_hi = sb("bc_hi", [P, CH, O], F32R)
        bc_lo = sb("bc_lo", [P, CH, O], F32R)
        gate_hl = sb("gate_hl", [P, CH, 2 * E], F32R)
        a_col = sb("a_col", [P, CH], F32)
        split = sb("split", [P, 2, 2, CH * GT], F32R)
        xnt_split = sb("xnt_split", [P, 2, CH * GT], F32R)
        SIZES = {"x": XR * TPG * D, "hs": 2 * CH * GT, "s": 2 * TPG * (O + 2), "w": WR * D}
        work = sb("work", [P, sum(SIZES.values())], F32)
        at = dict(zip(SIZES, np.cumsum([0, *SIZES.values()]).tolist()))

        def part(start, *shape):
            flat = work[:, start:start + int(np.prod(shape))]
            names = "abcd"[:len(shape)]
            if len(shape) == 1:
                return flat
            return flat.rearrange(f"p ({' '.join(names)}) -> p {' '.join(names)}", **dict(zip(names, shape)))

        x_sb = part(at["x"], XR, TPG, D)
        hs = part(at["hs"], 2, CH, GT)
        s_out = part(at["s"], 2, TPG, O + 2)
        w_stage = part(at["w"], WR, CH, P)
        hs_hi = [split[:, v, 0, :].rearrange("p (c n) -> p c n", c=CH) for v in range(2)]
        hs_lo = [split[:, v, 1, :].rearrange("p (c n) -> p c n", c=CH) for v in range(2)]
        xnt_hi, xnt_lo = [xnt_split[:, i, :].rearrange("p (c n) -> p c n", c=CH) for i in range(2)]
        gate_raw = work[0:E, at["hs"] + CH * GT:at["hs"] + CH * GT + D]
        bc_raw = part(at["s"], CH, O)
        empty_ids = part(at["x"] + (XR - 1) * TPG * D, TROWS).bitcast(I32)
        row_sb = part(0, RR, ROW)
        xn2 = part(RR * ROW, 2, D)
        o_sb = part(RR * ROW + 2 * D, OR, O)
        plan_at = RR * ROW + 2 * D + OR * O
        slot_tok = part(plan_at, TILES).bitcast(I32)
        e_row = part(plan_at + TILES, TILES).bitcast(I32)[0:1]
        assert plan_at >= at["w"] and plan_at + 2 * TILES <= sum(SIZES.values())
        blk_f = part(0, P)
        blk_i = part(P, P).bitcast(I32)
        past = part(2 * P, TILES, E)[0:1]
        e_row_f = part(2 * P + TILES * E, TILES)[0:1]
        x2_hi = [split[:, v, 0, 0:D] for v in range(2)]
        x2_lo = [split[:, v, 1, 0:D] for v in range(2)]
        ident = sb("ident", [P, P], F32)
        before = sb("before", [P, P], BF16)
        ones = sb("ones", [P, P], BF16)
        ones_f = sb("ones_f", [P, E], F32)
        score = sb("score", [P, TPG, E], F32)
        warm = sb("warm", [P, 1], F32)
        score_sb = sb("score_sb", [2 * E, GT], F32)
        prio = sb("prio", [P, TPG, E], F32)
        e_base = sb("e_base", [P, TPG, E], BF16)
        token_id = sb("token_id", [P, 4, TPG], I32)
        id_step = sb("id_step", [P, TPG], I32)
        stats = sb("stats", [P, 2, 6], F32)
        mv = sb("mv", [P, 4, TPG, 2], F32)
        std2 = sb("std2", [P, TPG], F32)
        half = sb("half", [P, TPG], F32)
        std = sb("std", [P, TPG], F32)
        shift = sb("shift", [P, 2, TPG], F32)
        eps_col = sb("eps_col", [P, 1], F32)
        top = sb("top", [P, TPG], F32)
        ranked = sb("ranked", [P, TPG, E], F32)
        first = sb("first", [P, TPG], F32)
        onehot = sb("onehot", [P, 2, TPG, E], BF16)
        placed = sb("placed", [P, TPG, E], F32)
        slot_id = sb("slot_id", [P, 4, TPG], I32)
        seen = sb("seen", [P, 2, TPG, E], BF16)
        tile_i = sb("tile_i", [P, 2, E], I32)
        tile_f = sb("tile_f", [P, E], F32)
        tile_cum = sb("tile_cum", [P, E], F32)
        done = sb("done", [P, E], F32)
        done_n = sb("done_n", [P, E], F32)
        j_col = sb("j_col", [P, 1], F32)
        j_row = sb("j_row", [P, TILES], F32)
        pick = sb("pick", [P, 4], F32)
        blk_row = sb("blk_row", [P, 1], I32)
        tok_in = sb("tok_in", [P, RR, 1], I32)
        tok_out = sb("tok_out", [P, OR, 1], I32)

        def bank(name, n=1):
            return ctx.enter_context(nc.psum_tensor(name, [P, n, 512], F32))

        ps_xt = bank("ps_xt", 2)
        ps_s = bank("ps_s", 4)
        ps_gate = bank("ps_gate")
        ps_w = bank("ps_w")
        xt_ps = ps_xt[:, :, :].rearrange("p a b -> p (a b)").rearrange("p (c n) -> p c n", c=CH)
        score_ps = ps_gate[:, 0, 0:TPG * 2 * E].rearrange("p (t e) -> p t e", t=TPG)
        rank_ps = ps_gate[:, 0, 32:32 + TPG * E].rearrange("p (t e) -> p t e", t=TPG)
        gate_ps = ps_gate[:, 0, 64:64 + CH * E].rearrange("p (c e) -> p c e", c=CH)
        count_ps = ps_gate[:, 0, 96:96 + E]
        slot_ps = ps_gate[:, 0, 128:128 + P]
        part_ps = ps_gate[0:2 * E, 0, 256:256 + GT]
        w_ps = ps_w[:, 0, :]
        x2_ps = [ps_xt[:, v, :] for v in range(2)]
        z_ps = [ps_s[:, v, :] for v in range(2)]
        g_ps = [ps_s[:, 2 + v, :] for v in range(2)]

        x_loaded = [sem(f"x_loaded{v}") for v in range(XR)]
        x_first = sem("x_first")
        x_copied = sem("x_copied")
        s_stored = [sem(f"s_stored{v}") for v in range(2)]
        a_loaded = sem("a_loaded")
        bc_loaded = sem("bc_loaded")
        gate_loaded = sem("gate_loaded")
        w_loaded = [sem(f"w_loaded{v}") for v in range(WR)]
        table_empty = sem("table_empty")
        id_stored = [sem(f"id_stored{u}") for u in range(4)]
        blk_loaded = sem("blk_loaded")
        row_loaded = [sem(f"row_loaded{u}") for u in range(RR)]
        out_stored = [sem(f"out_stored{u}") for u in range(OR)]
        const_ready = sem("const_ready")
        empty_ready = sem("empty_ready")
        bc_hi_done = sem("bc_hi_done")
        bc_last_hi = sem("bc_last_hi")
        bc_lo_done = sem("bc_lo_done")
        root_loaded = sem("root_loaded")
        silu_loaded = sem("silu_loaded")
        gate_turned = sem("gate_turned")
        gate_hi_done = sem("gate_hi_done")
        gate_ready = sem("gate_ready")
        stats_done = sem("stats_done")
        dev_step = sem("dev_step")
        var_ready = sem("var_ready")
        std_ready = sem("std_ready")
        shift_ready = sem("shift_ready")
        xn_ready = sem("xn_ready")
        xt_done = sem("xt_done")
        xnt_tail = sem("xnt_tail")
        xnt_head = sem("xnt_head")
        xnt_lo_done = sem("xnt_lo_done")
        scan_done = sem("scan_done")
        hi_done = sem("hi_done")
        lo_done = sem("lo_done")
        s_done = sem("s_done")
        s_taken = sem("s_taken")
        mv_taken = sem("mv_taken")
        mv_free = sem("mv_free")
        part_done = sem("part_done")
        part_copied = sem("part_copied")
        score_done = sem("score_done")
        gate_step = sem("gate_step")
        onehot_ready = sem("onehot_ready")
        seen_ready = sem("seen_ready")
        rank_done = sem("rank_done")
        slot_ready = sem("slot_ready")
        id_ready = sem("id_ready")
        w_ready = sem("w_ready")
        wt_done = sem("wt_done")
        w_hi_done = sem("w_hi_done")
        w_lo_done = sem("w_lo_done")
        count_done = sem("count_done")
        plan_step = sem("plan_step")
        blk_row_ready = sem("blk_row_ready")
        e_row_ready = sem("e_row_ready")
        blk_f_ready = sem("blk_f_ready")
        slot_turned = sem("slot_turned")
        slot_tok_ready = sem("slot_tok_ready")
        tok_in_ready = sem("tok_in_ready")
        tok_out_ready = sem("tok_out_ready")
        xn2_ready = sem("xn2_ready")
        x2_done = sem("x2_done")
        x2_hi_done = sem("x2_hi_done")
        x2_lo_done = sem("x2_lo_done")
        z_done = sem("z_done")
        silu_done = sem("silu_done")
        prod_done = sem("prod_done")
        o_ready = sem("o_ready")

        block = ctx.enter_context(nc.Block())

        def rounds(U, it, c, ring):
            return (U // ring) * it + c // ring

        def wait(engine, semaphore, count):
            if not (isinstance(count, int) and count <= 0):
                engine.wait_ge(semaphore, count)

        @block.sync
        def _(sp):
            def load_x(it, c):
                nc.sync.dma_start(x_sb[:, c % XR], x_g[4 * it + c]).then_inc(x_loaded[c % XR], 16)

            def next_x(it, c):
                sp.wait_ge(xt_done, 4 * it + c + 1)
                load_x(it, c + XR)

            def copy_x(it, c):
                nc.sync.dma_start(rows_g[4 * it + c][:, :, 0:D], x_g[4 * it + c]).then_inc(x_copied, 16)

            def store_s(it, c):
                sp.wait_ge(s_taken, TPG * (4 * it + c + 1))
                sp.wait_ge(mv_taken, 4 * it + c + 1)
                nc.sync.dma_start(rows_g[4 * it + c][:, :, D:ROW], s_out[:, c % 2]).then_inc(s_stored[c % 2], 16)

            def load_w(it, c):
                wait(sp, wt_done, 4 * it + c - WR + 1)
                nc.sync.dma_start(w_stage[:, c % WR], w_e[it + c // CH, c % CH]).then_inc(w_loaded[c % WR], 16)

            nc.sync.dma_start(x_sb[:, 0, 0], x_g[0][:, 0]).then_inc(x_first, 16)
            nc.sync.dma_start(x_sb[:, 0, 1:], x_g[0][:, 1:]).then_inc(x_loaded[0], 16)
            nc.sync.dma_start(gate_raw, gate_in).then_inc(gate_loaded, 16)
            with nc.allow_non_contiguous_dma(reason="512 decay factors, once"):
                nc.sync.dma_start(a_col[:, :], a_in.rearrange("(c p) -> p c", p=P)).then_inc(a_loaded, 16)
            load_x(0, 1)
            nc.sync.dma_start(bc_raw, bc_in.rearrange("(c p) o -> p c o", p=P)).then_inc(bc_loaded, 16)
            load_x(0, 2)
            for c in range(WR):
                load_w(0, c)
            sp.wait_ge(empty_ready, 1)
            nc.sync.dma_start(table.rearrange("(p r) q -> p (r q)", p=P), empty_ids).then_inc(table_empty, 16)
            sp.wait_ge(table_empty, 16)
            load_x(0, XR - 1)
            with sp.Fori(0, GROUPS // 4 - 1) as it:
                for c in range(4):
                    next_x(it, c)
                    copy_x(it, c)
                    load_w(it, c + WR)
                    store_s(it, c)
            for c in range(GROUPS - 4, GROUPS):
                if c + WR < BLOCKS:
                    load_w(0, c + WR)
                    for i in range(2):
                        copy_x(0, 2 * c - (GROUPS - 4) + i)
                if c < GROUPS - 1:
                    store_s(0, c)
            sp.wait_ge(mv_taken, GROUPS)
            for t in range(TPG):
                sp.wait_ge(s_taken, TPG * (GROUPS - 1) + t + 1)
                nc.sync.dma_start(rows_g[GROUPS - 1][:, t, D:ROW], s_out[:, LAST, t]).then_inc(s_stored[LAST], 16)

        @block.gpsimd
        def _(pool):
            nc.gpsimd.memset(empty_ids, EMPTY).then_inc(empty_ready, 1)
            nc.gpsimd.memset(ident[:, :], 0.0).then_inc(const_ready, 1)
            nc.gpsimd.memset(before[:, :], 1.0).then_inc(const_ready, 1)
            nc.gpsimd.memset(ones[:, :], 1.0).then_inc(const_ready, 1)
            nc.gpsimd.memset(ones_f[:, :], 1.0).then_inc(const_ready, 1)
            nc.gpsimd.memset(id_step[:, :], 4 * GT).then_inc(const_ready, 1)
            nc.gpsimd.memset(eps_col[:, :], 4 * EPS).then_inc(const_ready, 1)
            nc.gpsimd.memset(seen[:, 0], 0.0).then_inc(const_ready, 1)
            nc.gpsimd.iota(prio[:, :, :], [[0, TPG], [-1, E]], base=E, channel_multiplier=0,
                           allow_small_or_imprecise_dtypes=True).then_inc(const_ready, 1)
            nc.gpsimd.iota(e_base[:, :, :], [[0, TPG], [TOKENS // P, E]], base=0, channel_multiplier=0,
                           allow_small_or_imprecise_dtypes=True).then_inc(const_ready, 1)
            nc.gpsimd.iota(j_col[:, :], [[0, 1]], base=0, channel_multiplier=1,
                           allow_small_or_imprecise_dtypes=True).then_inc(const_ready, 1)
            nc.gpsimd.iota(j_row[:, :], [[1, TILES]], base=0, channel_multiplier=0,
                           allow_small_or_imprecise_dtypes=True).then_inc(const_ready, 1)
            nc.gpsimd.iota(token_id[:, :, :], [[GT, 4], [P, TPG]], base=-4 * GT,
                           channel_multiplier=1).then_inc(const_ready, 1)
            pool.wait_ge(const_ready, 12)
            nc.gpsimd.affine_select(out=ident[:, :], in_=ident[:, :], compare_op=ALU.not_equal, fill=1.0,
                                    base=0, pattern=[[-1, P]], channel_multiplier=1).then_inc(const_ready, 1)
            nc.gpsimd.affine_select(out=before[:, :], in_=before[:, :], compare_op=ALU.is_gt, fill=0.0,
                                    base=0, pattern=[[1, P]], channel_multiplier=-1).then_inc(const_ready, 1)
            pool.wait_ge(const_ready, 14)

            def add_identity(it, c):
                w = w_stage[:, c % WR, c % CH]
                pool.wait_ge(w_loaded[c % WR], 16 * (rounds(4, it, c, WR) + 1))
                nc.gpsimd.tensor_tensor(w, w, ident[:, :], ALU.add).then_inc(w_ready, 1)

            def count(it, c):
                pool.wait_ge(onehot_ready, 4 * it + c + 1)
                wait(pool, rank_done, 4 * it + c)
                wait(pool, seen_ready, 4 * it + c)
                nc.gpsimd.tensor_tensor(seen[:, (c + 1) % 2], seen[:, c % 2], onehot[:, c % 2],
                                        ALU.add).then_inc(seen_ready, 1)

            def low_part(it, c):
                pool.wait_ge(hi_done, 4 * it + c + 1)
                wait(pool, s_done, TPG * (4 * it + c - 1))
                nc.gpsimd.tensor_tensor(hs_lo[c % 2], hs[:, c % 2], hs_hi[c % 2],
                                        ALU.subtract).then_inc(lo_done, 1)

            def next_ids(it, c):
                u = c % 4
                wait(pool, id_stored[u], 32 * rounds(4, it, c, 4))
                nc.gpsimd.tensor_tensor(token_id[:, u], token_id[:, u], id_step[:, :], ALU.add).then_inc(id_ready, 1)

            def scatter_ids(it, c):
                u = c % 4
                pool.wait_ge(table_empty, 16)
                pool.wait_ge(id_ready, 4 * it + c + 1)
                pool.wait_ge(slot_ready, 4 * it + c + 1)
                for t in range(TPG):
                    nc.gpsimd.indirect_dma_start(
                        out=table_flat, out_offset=bass.IndirectOffsetOnAxis(ap=slot_id[:, u, t:t + 1], axis=0),
                        in_=token_id[:, u, t:t + 1], in_offset=None,
                        bounds_check=E * TOKENS - 1, oob_is_err=False).then_inc(id_stored[u], 16)

            pool.wait_ge(bc_loaded, 16)
            nc.gpsimd.tensor_copy(bc_hi[:, CH - 1], bc_raw[:, CH - 1]).then_inc(bc_last_hi, 1)
            pool.wait_ge(bc_last_hi, 1)
            nc.gpsimd.tensor_tensor(bc_lo[:, CH - 1], bc_raw[:, CH - 1], bc_hi[:, CH - 1],
                                    ALU.subtract).then_inc(bc_lo_done, 1)
            add_identity(0, 0)
            low_part(0, 0)
            next_ids(0, 0)
            add_identity(0, 1)

            def group(it, c, left=2):
                count(it, c)
                if left >= 1:
                    low_part(it, c + 1)
                    next_ids(it, c + 1)
                scatter_ids(it, c)
                if left >= 2:
                    add_identity(it, c + 2)

            for c in range(4):
                group(0, c)
            with pool.Fori(1, GROUPS // 4 - 1) as it:
                for c in range(4):
                    group(it, c)
            for c in range(GROUPS - 4, GROUPS):
                group(0, c, left=GROUPS - 1 - c)

            for u in range(4):
                pool.wait_ge(id_stored[u], 32 * (GROUPS // 4))
            pool.wait_ge(blk_row_ready, 1)
            nc.gpsimd.indirect_dma_start(
                out=blk_i, out_offset=None, in_=table,
                in_offset=bass.IndirectOffsetOnAxis(ap=blk_row[:, 0:1], axis=0),
                bounds_check=TROWS - 1, oob_is_err=False).then_inc(blk_loaded, 16)

            def gather(it, c):
                u = c % RR
                n = RR * it + c
                if not isinstance(it, int):
                    pool.to_reg(n - RR + 1)
                pool.wait_ge(x_copied, 16 * GROUPS)
                if isinstance(it, int) and n < RR:
                    pool.wait_ge(slot_tok_ready, 1)
                    tok = slot_tok[:, n:n + 1]
                else:
                    pool.wait_ge(tok_in_ready, n - RR + 1)
                    pool.wait_ge(o_ready, n - RR + 1)
                    tok = tok_in[:, u]
                nc.gpsimd.indirect_dma_start(
                    out=row_sb[:, u], out_offset=None, in_=rows,
                    in_offset=bass.IndirectOffsetOnAxis(ap=tok, axis=0),
                    bounds_check=TOKENS - 1, oob_is_err=False).then_inc(row_loaded[u], 16)

            def scatter(it, c):
                u = c % OR
                n = RR * it + c
                if not isinstance(it, int):
                    pool.to_reg(n + 1)
                pool.wait_ge(slot_tok_ready, 1)
                pool.wait_ge(tok_out_ready, n + 1)
                pool.wait_ge(o_ready, n + 1)
                nc.gpsimd.indirect_dma_start(
                    out=out_flat, out_offset=bass.IndirectOffsetOnAxis(ap=tok_out[:, u], axis=0),
                    in_=o_sb[:, u], in_offset=None,
                    bounds_check=TOKENS - 1, oob_is_err=False).then_inc(out_stored[u], 16)

            for v in range(2):
                pool.wait_ge(s_stored[v], 16 * (GROUPS // 2 + (TPG - 1 if v == LAST else 0)))
            for c in range(RR):
                gather(0, c)
            with pool.Fori(0, LOOPS) as it:
                for c in range(RR):
                    scatter(it, c)
                    gather(it, c + RR)
            for c in range(RR * LOOPS, TILES):
                scatter(0, c)
                if c + RR < TILES:
                    gather(0, c + RR)
            for u in range(OR):
                pool.wait_ge(out_stored[u], 16 * len(range(u, TILES, OR)))

        @block.scalar
        def _(act):
            def root(it, c):
                act.wait_ge(var_ready, 4 * it + c + 1)
                wait(act, shift_ready, 4 * it + c)
                nc.scalar.activation(std2[:, :], mv[:, c % 4, :, 1], ACT.Sqrt, bias=eps_col[:, 0:1],
                                     scale=4.0).then_inc(std_ready, 1)

            def normalise(it, c, t):
                if t == 0:
                    act.wait_ge(shift_ready, 4 * it + c + 1)
                xt = x_sb[:, c % XR, t]
                nc.scalar.activation(xt, xt, ACT.Identity, bias=shift[:, c % 2, t:t + 1],
                                     scale=mv[:, c % 4, t, 1:2]).then_inc(xn_ready, 1)

            def copy_tail(it, c):
                act.wait_ge(xt_done, 4 * it + c + 1)
                wait(act, part_done, 4 * it + c)
                nc.scalar.copy(xnt_hi[:, CH // 2:], xt_ps[:, CH // 2:]).then_inc(xnt_tail, 1)

            def copy_head(it, c):
                act.wait_ge(scan_done, CH * (4 * it + c) + CH // 2)
                nc.scalar.copy(xnt_hi[:, :CH // 2], xt_ps[:, :CH // 2]).then_inc(xnt_head, 1)

            def copy_parts(it, c):
                act.wait_ge(part_done, 4 * it + c + 1)
                wait(act, score_done, 4 * it + c)
                nc.scalar.copy(score_sb[:, :], part_ps).then_inc(part_copied, 1)

            def high_part(it, c):
                act.wait_ge(scan_done, CH * (4 * it + c + 1))
                wait(act, s_done, TPG * (4 * it + c - 1))
                nc.scalar.copy(hs_hi[c % 2], hs[:, c % 2]).then_inc(hi_done, 1)

            def block_high(it, c):
                act.wait_ge(wt_done, 4 * it + c + 1)
                nc.scalar.copy(w_hi[:, 4 * it + c], w_ps).then_inc(w_hi_done, 1)

            def take_s(it, c):
                v = c % 2
                wait(act, s_stored[v], 16 * rounds(4, it, c, 2))
                nc.scalar.copy(s_out[:, v, :, O:O + 2], mv[:, c % 4]).then_inc(mv_taken, 1)
                for t in range(TPG):
                    act.wait_ge(s_done, TPG * (4 * it + c) + t + 1)
                    nc.scalar.copy(s_out[:, v, t, 0:O], ps_s[:, 2 * v + t, :]).then_inc(s_taken, 1)

            act.wait_ge(const_ready, 14)
            nc.scalar.activation(warm[:, :], eps_col[:, 0:1], ACT.Sqrt).then_inc(root_loaded, 1)
            root(0, 0)
            act.wait_ge(gate_turned, 1)
            nc.scalar.copy(gate_hl[:, :, 0:E], gate_ps).then_inc(gate_hi_done, 1)
            normalise(0, 0, 0)
            normalise(0, 0, 1)
            root(0, 1)
            copy_tail(0, 0)
            copy_head(0, 0)
            act.wait_ge(bc_loaded, 16)
            nc.scalar.copy(bc_hi[:, :CH - 1], bc_raw[:, :CH - 1]).then_inc(bc_hi_done, 1)
            high_part(0, 0)
            copy_parts(0, 0)
            normalise(0, 1, 0)
            normalise(0, 1, 1)

            def group(it, c, left=3, start=False):
                if left >= LATE:
                    block_high(it, c)
                if left >= 1:
                    copy_tail(it, c + 1)
                    copy_head(it, c + 1)
                if not start:
                    take_s(it, c - 1)
                if left >= 1:
                    high_part(it, c + 1)
                if start:
                    root(0, 2)
                    copy_parts(0, 1)
                if left >= 2:
                    normalise(it, c + 2, 0)
                if left >= 1 and not start:
                    copy_parts(it, c + 1)
                if left >= 2:
                    normalise(it, c + 2, 1)
                if left >= 3:
                    root(it, c + 3)

            for c in range(4):
                group(0, c, start=(c == 0))
            with act.Fori(1, GROUPS // 4 - 1) as it:
                for c in range(4):
                    group(it, c)
            for c in range(GROUPS - 4, GROUPS):
                group(0, c, left=GROUPS - 1 - c)
            take_s(0, GROUPS - 1)
            for c in range(GROUPS - LATE, GROUPS):
                block_high(0, c)
            act.wait_ge(root_loaded, 1)
            nc.scalar.activation(warm[:, :], eps_col[:, 0:1], ACT.Silu).then_inc(silu_loaded, 1)

            def high_x2(it, c):
                act.wait_ge(x2_done, RR * it + c + 1)
                wait(act, z_done, RR * it + c - 1)
                nc.scalar.copy(x2_hi[c % 2], x2_ps[c % 2]).then_inc(x2_hi_done, 1)

            def silu(it, c):
                act.wait_ge(z_done, RR * it + c + 1)
                wait(act, prod_done, RR * it + c - 1)
                nc.scalar.activation(g_ps[c % 2], z_ps[c % 2], ACT.Silu).then_inc(silu_done, 1)

            def ids_in(it, c):
                wait(act, row_loaded[c % RR], 16 * rounds(RR, it, c, RR))
                nc.scalar.copy(tok_in[:, c % RR], slot_tok[:, bass.ds(RR * it + c, 1)]).then_inc(tok_in_ready, 1)

            def ids_out(it, c):
                wait(act, out_stored[c % OR], 16 * rounds(RR, it, c, OR))
                nc.scalar.copy(tok_out[:, c % OR], slot_tok[:, bass.ds(RR * it + c, 1)]).then_inc(tok_out_ready, 1)

            def tile(it, c, ahead=True):
                silu(it, c)
                high_x2(it, c + 2)
                ids_out(it, c)
                if ahead:
                    ids_in(it, c + RR)

            act.wait_ge(slot_tok_ready, 1)
            high_x2(0, 0)
            high_x2(0, 1)
            for c in range(RR):
                tile(0, c)
            with act.Fori(1, LOOPS) as it:
                for c in range(RR):
                    tile(it, c)
            for c in range(RR * LOOPS, TILES - 2):
                tile(0, c, ahead=c + RR < TILES)
            for c in range(TILES - 2, TILES):
                silu(0, c)
                ids_out(0, c)

        @block.vector
        def _(dve):
            U = GPB

            def statistics(it, c, start=False):
                if start:
                    dve.wait_ge(x_first, 16)
                else:
                    dve.wait_ge(x_loaded[c % XR], 16 * (rounds(U, it, c, XR) + 1))
                for t in range(TPG):
                    if start and t == 1:
                        dve.wait_ge(x_loaded[0], 16)
                    last = nc.vector.bn_stats(stats[:, t, :], x_sb[:, c % XR, t])
                last.then_inc(stats_done, 1)

            def variance(it, c):
                for t in range(TPG):
                    last = nc.vector.bn_aggr(mv[:, c % 4, t], stats[:, t, :])
                last.then_inc(var_ready, 1)

            def scan(it, c):
                n = U * it + c
                v = c % 2
                dve.wait_ge(xt_done, n + 1)
                wait(dve, lo_done, n - 1)
                wait(dve, scan_done, CH * n)
                for k in range(CH):
                    if k == CH // 2:
                        dve.wait_ge(xnt_tail, n + 1)
                    start = 0.0 if c % GPB == 0 else hs[:, 1 - v, k, GT - 1:GT]
                    nc.vector.tensor_tensor_scan(hs[:, v, k, :], a_col[:, k:k + 1].to_broadcast([P, GT]),
                                                 xt_ps[:, k, :], start, ALU.mult, ALU.add).then_inc(scan_done, 1)

            def deviation(it, c, step):
                n = U * it + c
                m = mv[:, c % 4]
                if step == 0:
                    dve.wait_ge(std_ready, n + 1)
                    nc.vector.reciprocal(half[:, :], std2[:, :]).then_inc(dev_step, 1)
                elif step == 1:
                    dve.wait_ge(dev_step, 4 * n + 1)
                    nc.vector.scalar_tensor_tensor(half[:, :], m[:, :, 1], EPS, half[:, :], ALU.add,
                                                   ALU.mult).then_inc(dev_step, 1)
                elif step == 2:
                    dve.wait_ge(dev_step, 4 * n + 2)
                    nc.vector.scalar_tensor_tensor(std[:, :], std2[:, :], 0.25, half[:, :], ALU.mult,
                                                   ALU.add).then_inc(dev_step, 1)
                elif step == 3:
                    dve.wait_ge(dev_step, 4 * n + 3)
                    nc.vector.reciprocal(m[:, :, 1], std[:, :]).then_inc(dev_step, 1)
                else:
                    dve.wait_ge(dev_step, 4 * n + 4)
                    wait(dve, xn_ready, TPG * (n - 1))
                    nc.vector.scalar_tensor_tensor(shift[:, c % 2], m[:, :, 0], -1.0, m[:, :, 1], ALU.mult,
                                                   ALU.mult).then_inc(shift_ready, 1)

            def low_xnt(it, c):
                n = U * it + c
                dve.wait_ge(xnt_head, n + 1)
                wait(dve, part_done, n)
                nc.vector.tensor_tensor(xnt_lo, xt_ps, xnt_hi, ALU.subtract).then_inc(xnt_lo_done, 1)

            def place(it, c, step):
                n = U * it + c
                u = c % 4
                if step == 0:
                    dve.wait_ge(rank_done, n + 1)
                    nc.vector.tensor_tensor(placed[:, :, :], rank_ps, onehot[:, c % 2], ALU.mult).then_inc(gate_step, 1)
                else:
                    dve.wait_ge(gate_step, 5 * n + 5)
                    wait(dve, id_stored[u], 32 * rounds(U, it, c, 4))
                    with nc.allow_low_precision(reason="one whole number below 2**24 and zeros: the sum is exact"):
                        nc.vector.tensor_reduce(slot_id[:, u], placed[:, :, :], AX.X, ALU.add).then_inc(slot_ready, 1)

            def route(it, c, ahead, behind=True):
                n = U * it + c
                v = c % 2
                if ahead:
                    deviation(it, c + 2, 0)
                dve.wait_ge(score_done, n + 1)
                if behind:
                    place(it, c - 1, 0)
                nc.vector.tensor_reduce(score[:, :, :], score_ps.rearrange("p t (i e) -> p t e i", e=E), AX.X,
                                        ALU.add).then_inc(gate_step, 1)
                if behind:
                    place(it, c - 1, 1)
                if ahead:
                    deviation(it, c + 2, 1)
                dve.wait_ge(gate_step, 5 * n + 1)
                nc.vector.tensor_reduce(top[:, :], score[:, :, :], AX.X, ALU.max).then_inc(gate_step, 1)
                if ahead:
                    deviation(it, c + 2, 2)
                dve.wait_ge(gate_step, 5 * n + 2)
                for t in range(TPG):
                    last = nc.vector.scalar_tensor_tensor(ranked[:, t], score[:, t], top[:, t:t + 1],
                                                          prio[:, t], ALU.is_equal, ALU.mult)
                last.then_inc(gate_step, 1)
                if ahead:
                    deviation(it, c + 2, 3)
                dve.wait_ge(gate_step, 5 * n + 3)
                nc.vector.tensor_reduce(first[:, :], ranked[:, :, :], AX.X, ALU.max).then_inc(gate_step, 1)
                if ahead:
                    deviation(it, c + 2, 4)
                dve.wait_ge(gate_step, 5 * n + 4)
                wait(dve, rank_done, n - 1)
                wait(dve, seen_ready, n - 1)
                for t in range(TPG):
                    last = nc.vector.tensor_scalar(onehot[:, v, t], ranked[:, t], first[:, t:t + 1], None,
                                                   ALU.is_equal)
                last.then_inc(onehot_ready, 1)

            def block_low(it, c):
                n = U * it + c
                dve.wait_ge(w_hi_done, n + 1)
                nc.vector.tensor_tensor(w_lo[:, n], w_ps, w_hi[:, n], ALU.subtract).then_inc(w_lo_done, 1)

            for c in range(2):
                statistics(0, c, start=(c == 0))
                dve.wait_ge(stats_done, c + 1)
                variance(0, c)
                for step in range(5):
                    deviation(0, c, step)
                if c == 0:
                    dve.wait_ge(gate_hi_done, 1)
                    nc.vector.tensor_tensor(gate_hl[:, :, E:2 * E], gate_ps, gate_hl[:, :, 0:E],
                                            ALU.subtract).then_inc(gate_ready, 1)
            dve.wait_ge(const_ready, 14)
            dve.wait_ge(a_loaded, 16)
            scan(0, 0)
            low_xnt(0, 0)
            dve.wait_ge(bc_hi_done, 1)
            nc.vector.tensor_tensor(bc_lo[:, :CH - 1], bc_raw[:, :CH - 1], bc_hi[:, :CH - 1],
                                    ALU.subtract).then_inc(bc_lo_done, 1)
            route(0, 0, False, behind=False)

            def group(it, c, left=3, start=False):
                if left >= 1:
                    scan(it, c + 1)
                    low_xnt(it, c + 1)
                if start:
                    statistics(0, 2)
                    dve.wait_ge(stats_done, 3)
                    variance(0, 2)
                if left == 0:
                    place(it, c, 0)
                    place(it, c, 1)
                if left >= LATE:
                    block_low(it, c)
                if start:
                    for step in range(5):
                        deviation(0, 2, step)
                if left >= 3:
                    statistics(it, c + 3)
                    dve.wait_ge(stats_done, U * it + c + 4)
                    wait(dve, mv_taken, U * it + c)
                    dve.sem_inc(mv_free, 1)
                    variance(it, c + 3)
                if left >= 1:
                    route(it, c + 1, left >= 3)

            for c in range(GPB):
                group(0, c, start=(c == 0))
            with dve.Fori(1, BATCH - 1) as b:
                for c in range(GPB):
                    group(b, c)
            for c in range(GROUPS - GPB, GROUPS):
                group(0, c, left=GROUPS - 1 - c)

            def step(ins, k):
                ins.then_inc(plan_step, 1)
                dve.wait_ge(plan_step, k)

            dve.wait_ge(count_done, 1)
            step(nc.vector.tensor_scalar(tile_i[:, 0], count_ps, float(P - 1), None, ALU.add), 1)
            step(nc.vector.tensor_scalar(tile_i[:, 1], tile_i[:, 0], P.bit_length() - 1, None,
                                         ALU.logical_shift_right), 2)
            step(nc.vector.tensor_copy(tile_f[:, :], tile_i[:, 1]), 3)
            step(nc.vector.tensor_tensor_scan(tile_cum[:, :], ones_f[:, :], tile_f[:, :], 0.0, ALU.mult, ALU.add), 4)
            step(nc.vector.tensor_scalar(done[:, :], tile_cum[:, :], j_col[:, 0:1], None, ALU.is_le), 5)
            nc.vector.tensor_reduce(pick[:, 0:1], done[:, :], AX.X, ALU.add)
            step(nc.vector.tensor_tensor(done_n[:, :], done[:, :], tile_f[:, :], ALU.mult), 6)
            step(nc.vector.tensor_reduce(pick[:, 1:2], done_n[:, :], AX.X, ALU.add), 7)
            step(nc.vector.tensor_scalar(pick[:, 2:3], pick[:, 0:1], float(TOKENS // P), j_col[:, 0:1],
                                         ALU.mult, ALU.add), 8)
            nc.vector.tensor_tensor(blk_row[:, :], pick[:, 2:3], pick[:, 1:2], ALU.subtract).then_inc(blk_row_ready, 1)
            step(nc.vector.tensor_tensor(
                past, tile_cum[0:1, :].unsqueeze(1).to_broadcast([1, TILES, E]),
                j_row[0:1, :].unsqueeze(2).to_broadcast([1, TILES, E]), ALU.is_le), 9)
            step(nc.vector.tensor_reduce(e_row_f[:, :], past, AX.X, ALU.add), 10)
            nc.vector.tensor_scalar(e_row[:, :], e_row_f[:, :], float(E - 1), None, ALU.min).then_inc(e_row_ready, 1)
            for c in range(GROUPS - LATE, GROUPS - 1):
                block_low(0, c)
            dve.wait_ge(blk_loaded, 16)
            nc.vector.tensor_copy(blk_f, blk_i).then_inc(blk_f_ready, 1)
            dve.wait_ge(slot_turned, 1)
            nc.vector.tensor_copy(slot_tok[:, :], slot_ps[:, 0:TILES]).then_inc(slot_tok_ready, 1)
            block_low(0, GROUPS - 1)

            def normalise(it, c):
                row = row_sb[:, c % RR]
                dve.wait_ge(row_loaded[c % RR], 16 * (rounds(RR, it, c, RR) + 1))
                wait(dve, x2_done, RR * it + c - 1)
                nc.vector.tensor_scalar(xn2[:, c % 2], row[:, 0:D], row[:, D + O:D + O + 1], row[:, D + O + 1:ROW],
                                        ALU.subtract, ALU.mult).then_inc(xn2_ready, 1)

            def low_x2(it, c):
                dve.wait_ge(x2_hi_done, RR * it + c + 1)
                nc.vector.tensor_tensor(x2_lo[c % 2], x2_ps[c % 2], x2_hi[c % 2],
                                        ALU.subtract).then_inc(x2_lo_done, 1)

            def product(it, c):
                dve.wait_ge(silu_done, RR * it + c + 1)
                wait(dve, out_stored[c % OR], 16 * rounds(RR, it, c, OR))
                nc.vector.tensor_tensor(o_sb[:, c % OR], row_sb[:, c % RR, D:D + O], g_ps[c % 2],
                                        ALU.mult).then_inc(prod_done, 1)

            def residual(it, c):
                dve.wait_ge(prod_done, RR * it + c + 1)
                nc.vector.tensor_tensor(o_sb[:, c % OR], o_sb[:, c % OR], row_sb[:, c % RR, 0:D],
                                        ALU.add).then_inc(o_ready, 1)

            def tile(it, c, ahead=3):
                if ahead >= 3:
                    normalise(it, c + 3)
                if ahead >= 2:
                    low_x2(it, c + 2)
                product(it, c)
                residual(it, c)

            normalise(0, 0)
            normalise(0, 1)
            low_x2(0, 0)
            normalise(0, 2)
            low_x2(0, 1)
            for c in range(RR):
                tile(0, c)
            with dve.Fori(1, LOOPS) as it:
                for c in range(RR):
                    tile(it, c)
            for c in range(RR * LOOPS, TILES):
                tile(0, c, ahead=TILES - 1 - c)

        @block.tensor
        def _(pe):
            pe.wait_ge(const_ready, 14)

            def turn_x(it, c):
                wait(pe, scan_done, CH * (4 * it + c))
                wait(pe, xnt_lo_done, 4 * it + c)
                for t in range(TPG):
                    pe.wait_ge(xn_ready, TPG * (4 * it + c) + t + 1)
                    for k in range(CH):
                        last = nc.tensor.transpose(xt_ps[:, k, t * P:(t + 1) * P],
                                                   x_sb[:, c % XR, t, k * P:(k + 1) * P], ident[:, :])
                last.then_inc(xt_done, 1)

            def score_parts(it, c):
                pe.wait_ge(xnt_lo_done, 4 * it + c + 1)
                wait(pe, slot_ready, 4 * it + c - 1)
                wait(pe, onehot_ready, 4 * it + c)
                for k in range(CH):
                    nc.tensor.matmul(part_ps, gate_hl[:, k], xnt_hi[:, k], start=(k == 0), stop=False)
                    last = nc.tensor.matmul(part_ps, gate_hl[:, k], xnt_lo[:, k], start=False, stop=(k == CH - 1))
                last.then_inc(part_done, 1)

            def scores(it, c):
                for t in range(TPG):
                    last = nc.tensor.transpose(score_ps[:, t], score_sb[:, t * P:(t + 1) * P],
                                               ident[0:2 * E, 0:2 * E])
                last.then_inc(score_done, 1)

            def ranks(it, c, more=True):
                pe.wait_ge(onehot_ready, 4 * it + c + 1)
                wait(pe, seen_ready, 4 * it + c)
                wait(pe, slot_ready, 4 * it + c)
                if more:
                    pe.wait_ge(part_copied, 4 * it + c + 2)
                nc.tensor.matmul(rank_ps, ones[:, :], e_base[:, :, :], start=True, stop=False)
                for i in range(TPG):
                    nc.tensor.matmul(rank_ps, ones[:, :], seen[:, c % 2, i].unsqueeze(1).to_broadcast([P, TPG, E]),
                                     start=False, stop=False)
                for t in range(1, TPG):
                    for i in range(t):
                        nc.tensor.matmul(rank_ps[:, t], ones[:, :], onehot[:, c % 2, i], start=False, stop=False)
                last = nc.tensor.matmul(rank_ps, before[:, :], onehot[:, c % 2], start=False, stop=True)
                last.then_inc(rank_done, 1)

            def turn_w(it, c):
                pe.wait_ge(w_ready, 4 * it + c + 1)
                wait(pe, w_lo_done, 4 * it + c)
                for f in range(CH):
                    last = nc.tensor.transpose(w_ps[:, f * P:(f + 1) * P], w_stage[:, c % WR, f],
                                               ident[:, :])
                last.then_inc(wt_done, 1)

            def product_hi(it, c, t):
                v = c % 2
                if t == 0:
                    pe.wait_ge(hi_done, 4 * it + c + 1)
                    wait(pe, s_taken, TPG * (4 * it + c - 1))
                for k in range(CH):
                    left = hs_hi[v][:, k, t * P:(t + 1) * P]
                    nc.tensor.matmul(ps_s[:, 2 * v + t], left, bc_hi[:, k], start=(k == 0), stop=False)
                    nc.tensor.matmul(ps_s[:, 2 * v + t], left, bc_lo[:, k], start=False, stop=False)

            def product_lo(it, c, t):
                v = c % 2
                pe.wait_ge(lo_done, 4 * it + c + 1)
                for k in range(CH):
                    last = nc.tensor.matmul(ps_s[:, 2 * v + t], hs_lo[v][:, k, t * P:(t + 1) * P], bc_hi[:, k],
                                            start=False, stop=(k == CH - 1))
                last.then_inc(s_done, 1)

            def keep_warm(idle_bank, times):
                for _ in range(times):
                    nc.tensor.transpose(idle_bank[:, 0:P], ident[:, :], ident[:, :])

            keep_warm(ps_s[:, 3], 4)
            pe.wait_ge(gate_loaded, 16)
            for k in range(CH):
                last = nc.tensor.transpose(gate_ps[:, k], gate_raw[:, k * P:(k + 1) * P], ident[0:E, 0:E])
            last.then_inc(gate_turned, 1)
            keep_warm(ps_s[:, 3], 17)
            turn_x(0, 0)
            keep_warm(ps_s[:, 3], 28)
            pe.wait_ge(gate_ready, 1)
            score_parts(0, 0)
            pe.wait_ge(part_copied, 1)
            scores(0, 0)
            turn_w(0, 0)
            turn_x(0, 1)
            pe.wait_ge(bc_lo_done, 2)

            def group(it, c, turned=False, weights=True):
                if not turned:
                    turn_x(it, c + 1)
                product_hi(it, c, 0)
                product_hi(it, c, 1)
                score_parts(it, c + 1)
                product_lo(it, c, 0)
                ranks(it, c)
                scores(it, c + 1)
                product_lo(it, c, 1)
                if weights:
                    turn_w(it, c + 1)

            for c in range(4):
                group(0, c, turned=(c == 0))
            with pe.Fori(1, GROUPS // 4 - 1) as it:
                for c in range(4):
                    group(it, c)
            for c in range(GROUPS - 4, GROUPS - 1):
                group(0, c, weights=c + 1 < GROUPS - LATE)
            ranks(0, GROUPS - 1, more=False)
            product_hi(0, GROUPS - 1, 0)
            pe.wait_ge(seen_ready, GROUPS)
            pe.wait_ge(slot_ready, GROUPS)
            for i in range(TPG):
                last = nc.tensor.matmul(count_ps, ones[:, :], seen[:, GROUPS % 2, i], start=(i == 0),
                                        stop=(i == TPG - 1))
            last.then_inc(count_done, 1)
            product_lo(0, GROUPS - 1, 0)
            product_hi(0, GROUPS - 1, 1)
            product_lo(0, GROUPS - 1, 1)
            for c in range(GROUPS - LATE, GROUPS):
                turn_w(0, c)
                keep_warm(x2_ps[0], 13)
            pe.wait_ge(blk_f_ready, 1)
            nc.tensor.transpose(slot_ps, blk_f, ident[:, :]).then_inc(slot_turned, 1)
            keep_warm(x2_ps[0], 46)

            def turn_x2(it, c):
                v = c % 2
                pe.wait_ge(xn2_ready, RR * it + c + 1)
                wait(pe, x2_lo_done, RR * it + c - 1)
                for k in range(CH):
                    last = nc.tensor.transpose(x2_ps[v][:, k * P:(k + 1) * P], xn2[:, v, k * P:(k + 1) * P],
                                               ident[:, :])
                last.then_inc(x2_done, 1)

            def expert(it, c, e):
                v = c % 2
                pe.wait_ge(x2_lo_done, RR * it + c + 1)
                wait(pe, silu_done, RR * it + c - 1)
                for k in range(CH):
                    hi, lo = x2_hi[v][:, k * P:(k + 1) * P], x2_lo[v][:, k * P:(k + 1) * P]
                    wh, wl = w_hi[:, e * CH + k], w_lo[:, e * CH + k]
                    nc.tensor.matmul(z_ps[v], hi, wh, start=(k == 0), stop=False)
                    nc.tensor.matmul(z_ps[v], hi, wl, start=False, stop=False)
                    last = nc.tensor.matmul(z_ps[v], lo, wh, start=False, stop=(k == CH - 1))
                last.then_inc(z_done, 1)

            def tile(it, c, ahead=True):
                e = nc.tensor.value_load(e_row[0:1, bass.ds(RR * it + c, 1)], min_val=0, max_val=E - 1)
                if ahead:
                    turn_x2(it, c + 1)
                expert(it, c, e)

            pe.wait_ge(e_row_ready, 1)
            pe.wait_ge(w_lo_done, BLOCKS)
            turn_x2(0, 0)
            for c in range(RR):
                tile(0, c)
            with pe.Fori(1, LOOPS) as it:
                for c in range(RR):
                    tile(it, c)
            for c in range(RR * LOOPS, TILES):
                tile(0, c, ahead=c + 1 < TILES)


_INS = ["L0_attn_inputs", "L0_attn_A", "L0_attn_BC", "L0_ffn_gate_w", "L0_ffn_expert_w"]


def kernel(**inputs):
    import numpy as _np
    import concourse.bacc as _bacc
    from concourse import mybir as _mybir
    from concourse.bass_utils import run_bass_kernel_spmd as _run

    nc = _bacc.Bacc("TRN2", target_bir_lowering=False, num_devices=1)
    arrays, args = {}, []
    for name in _INS:
        a = _np.ascontiguousarray(inputs[name])
        arrays[f"in_{name}_dram"] = a
        args.append(nc.dram_tensor(f"in_{name}_dram", a.shape, _mybir.dt.from_np(a.dtype), kind="ExternalInput").ap())
    shape = inputs["L0_attn_inputs"].shape
    out = nc.dram_tensor("out_0_dram", shape, _mybir.dt.float32, kind="ExternalOutput").ap()
    bass_recurrent_routed(nc, *args, out)
    r = _run(nc, [arrays], core_ids=[0])
    return r.results[0]["out_0_dram"]
```
